# Optimizing a Trainium2 kernel written in Bass

```python
import numpy as np
import jax
import jax.numpy as jnp

def _softmax(x, axis=-1):
    return jax.nn.softmax(x, axis=axis)

def _gelu(x):
    return jax.nn.gelu(x, approximate=True)

def _silu(x):
    return jax.nn.silu(x)

def _sigmoid(x):
    return jax.nn.sigmoid(x)

def _layernorm(x, axis=-1, eps=1e-05):
    m = jnp.mean(x, axis=axis, keepdims=True)
    v = jnp.var(x, axis=axis, keepdims=True)
    return (x - m) / jnp.sqrt(v + eps)

def _scatter_add(tgt, idx, src, axis=0):
    return tgt.at[idx].add(src)

def _segment_sum(src, seg, n):
    return jax.ops.segment_sum(src, seg, n)
kernel_name = 'mk_xattn_ffn_d1_seqx_r4_cb4810'

def setup_inputs(seed: int=0):
    np.random.seed(seed)
    _w = jnp.asarray

    def _rec_inputs():
        import jax
        import jax.numpy as jnp
        _rk = jax.random.key(seed)
        x = 7.22e-05 + 1 * jax.random.normal(jax.random.fold_in(_rk, 1), (16, 256, 256), jnp.float32)
        _lenS = 256 - jax.random.randint(jax.random.fold_in(_rk, 7), (16,), 0, max(1, 256 // 4) + 1, jnp.int32)
        _lenS2 = 256 - jax.random.randint(jax.random.fold_in(_rk, 8), (16,), 0, max(1, 256 // 4) + 1, jnp.int32)
        _ctx_1024P = jax.random.normal(jax.random.fold_in(_rk, 11), (16, 16, 256), jnp.float32)
        _ctx_1024c = jax.random.dirichlet(jax.random.fold_in(_rk, 511), 0.3 * jnp.ones((16,), jnp.float32), (16, 256))
        _ctx_1024t = jnp.einsum('bsk,bkd->bsd', _ctx_1024c, _ctx_1024P)
        _ctx_1024t = _ctx_1024t * jax.lax.rsqrt(jnp.mean(jnp.square(_ctx_1024t)) + 1e-12) * 0.953939
        ctx_1024 = 4.13588e-05 + 0.999923 * (_ctx_1024t + 0.3 * jax.random.normal(jax.random.fold_in(_rk, 611), (16, 256, 256), jnp.float32))
        _validS = jnp.arange(256)[None, :] < _lenS[:, None]
        _validS2 = jnp.arange(256)[None, :] < _lenS2[:, None]
        _causal = jnp.tril(jnp.ones((256, 256), dtype=bool))
        mask_BxS2_bf1 = jnp.ones((16, 256), dtype=bool)
        mask_BxS2_bk0 = jnp.logical_not(jnp.broadcast_to(_validS2[:, :], (16, 256)))
        return (x, ctx_1024, mask_BxS2_bf1, mask_BxS2_bk0)
    x, ctx_1024, mask_BxS2_bf1, mask_BxS2_bk0 = _rec_inputs()

    def _L0_xattn_setup():
        import jax, jax.numpy as jnp
        import numpy as np
        D_MODEL = 256
        N_HEADS = 16
        NUM_KV_HEADS = 4
        D_K = D_MODEL // N_HEADS
        ROPE_BASE = 10000.0

        def _apply_rope(x, dim, base=ROPE_BASE, position_offset=0):
            T = x.shape[2]
            dtype = x.dtype
            theta = base ** (-jnp.arange(0, dim, 2, dtype=dtype) / dim)
            positions = jnp.arange(position_offset, position_offset + T, dtype=dtype)[:, None]
            angles = positions * theta[None, :]
            sin = jnp.sin(angles)[None, None]
            cos = jnp.cos(angles)[None, None]
            x1 = x[..., :dim // 2]
            x2 = x[..., dim // 2:dim]
            return jnp.concatenate([x1 * cos - x2 * sin, x1 * sin + x2 * cos], axis=-1)
        key = jax.random.key(seed)
        ks = jax.random.split(key, 7)
        B, Tq, Tkv = (4, 512, 512)
        s = 1.0 / np.sqrt(D_MODEL)
        return {'query': jax.random.normal(ks[0], (B, Tq, D_MODEL), jnp.float32), 'key_value': jax.random.normal(ks[1], (B, Tkv, D_MODEL), jnp.float32), 'query_mask': jnp.ones((B, Tq), dtype=bool), 'kv_mask': jax.random.randint(ks[2], (B, Tkv), 0, 2) > 0, 'w_q': jax.random.normal(ks[3], (D_MODEL, D_MODEL), jnp.float32) * s, 'w_k': jax.random.normal(ks[4], (D_MODEL, NUM_KV_HEADS * D_K), jnp.float32) * s, 'w_v': jax.random.normal(ks[5], (D_MODEL, NUM_KV_HEADS * D_K), jnp.float32) * s, 'w_out': jax.random.normal(ks[6], (D_MODEL, D_MODEL), jnp.float32) * s}
    _L0_xattn_all = _L0_xattn_setup()
    _L0_xattn_in = {k: v for k, v in _L0_xattn_all.items() if k in ('w_q', 'w_k', 'w_v', 'w_out')}
    del _L0_xattn_all

    def _L0_ffn_setup():
        import jax, jax.numpy as jnp
        import numpy as np
        from jax import lax
        B, L, D = (4, 512, 256)
        E, TOPK = (8, 2)
        K, DIL = (3, 1)
        HID = D // 4
        EPS = 1e-06

        def _rmsnorm(h, w):
            rms = jnp.sqrt(jnp.mean(h * h, axis=-1, keepdims=True) + EPS)
            return w * (h / rms)

        def _forward(x, dw_kernel, dw_bias, pw_w, pw_b, router_w, router_b, expert_w, expert_b, out_w, out_b, norm_w, ff_down_w, ff_down_b, ff_up_w, ff_up_b):
            pad = (K - 1) * DIL
            xc = jnp.transpose(x, (0, 2, 1))
            xc = lax.conv_general_dilated(xc, dw_kernel, window_strides=(1,), padding=((pad, 0),), rhs_dilation=(DIL,), dimension_numbers=('NCH', 'OIH', 'NCH'), feature_group_count=D) + dw_bias[None, :, None]
            xc = jax.nn.silu(jnp.einsum('bdl,ed->bel', xc, pw_w) + pw_b[None, :, None])
            x1 = x + jnp.transpose(xc, (0, 2, 1))
            logits = jnp.einsum('bsd,ed->bse', x1, router_w) + router_b
            top_v, top_i = lax.top_k(logits, TOPK)
            top_w = jax.nn.softmax(top_v, axis=-1)
            rw = jnp.sum(jax.nn.one_hot(top_i, E, dtype=x1.dtype) * top_w[..., None], axis=-2)
            ye = jax.nn.silu(jnp.einsum('bsd,eod->bseo', x1, expert_w) + expert_b)
            combined = jnp.einsum('bse,bseo->bso', rw, ye)
            moe_out = jnp.einsum('bsd,od->bso', combined, out_w) + out_b
            h = _rmsnorm(x1 + moe_out, norm_w)
            ff = jax.nn.gelu(jnp.einsum('bsd,hd->bsh', h, ff_down_w) + ff_down_b, approximate=False)
            ff = jnp.einsum('bsh,dh->bsd', ff, ff_up_w) + ff_up_b
            return h + ff
        key = jax.random.key(seed)
        ks = jax.random.split(key, 16)
        s = 0.02
        return {'x': jax.random.normal(ks[0], (B, L, D), dtype=jnp.float32), 'dw_kernel': jax.random.normal(ks[1], (D, 1, K), dtype=jnp.float32) * s, 'dw_bias': jnp.zeros((D,), dtype=jnp.float32), 'pw_w': jax.random.normal(ks[2], (D, D), dtype=jnp.float32) * s, 'pw_b': jnp.zeros((D,), dtype=jnp.float32), 'router_w': jax.random.normal(ks[3], (E, D), dtype=jnp.float32) * s, 'router_b': jnp.zeros((E,), dtype=jnp.float32), 'expert_w': jax.random.normal(ks[4], (E, D, D), dtype=jnp.float32) * s, 'expert_b': jnp.zeros((E, D), dtype=jnp.float32), 'out_w': jax.random.normal(ks[5], (D, D), dtype=jnp.float32) * s, 'out_b': jnp.zeros((D,), dtype=jnp.float32), 'norm_w': jnp.ones((D,), dtype=jnp.float32), 'ff_down_w': jax.random.normal(ks[6], (HID, D), dtype=jnp.float32) * s, 'ff_down_b': jnp.zeros((HID,), dtype=jnp.float32), 'ff_up_w': jax.random.normal(ks[7], (D, HID), dtype=jnp.float32) * s, 'ff_up_b': jnp.zeros((D,), dtype=jnp.float32)}
    _L0_ffn_all = _L0_ffn_setup()
    _L0_ffn_in = {k: v for k, v in _L0_ffn_all.items() if k in ('dw_kernel', 'dw_bias', 'pw_w', 'pw_b', 'router_w', 'router_b', 'expert_w', 'expert_b', 'out_w', 'out_b', 'norm_w', 'ff_down_w', 'ff_down_b', 'ff_up_w', 'ff_up_b')}
    del _L0_ffn_all
    return {'x': x, 'ctx_1024': ctx_1024, 'mask_BxS2_bf1': mask_BxS2_bf1, 'mask_BxS2_bk0': mask_BxS2_bk0, 'L0_xattn_w_q': _L0_xattn_in['w_q'], 'L0_xattn_w_k': _L0_xattn_in['w_k'], 'L0_xattn_w_v': _L0_xattn_in['w_v'], 'L0_xattn_w_out': _L0_xattn_in['w_out'], 'L0_ffn_dw_kernel': _L0_ffn_in['dw_kernel'], 'L0_ffn_dw_bias': _L0_ffn_in['dw_bias'], 'L0_ffn_pw_w': _L0_ffn_in['pw_w'], 'L0_ffn_pw_b': _L0_ffn_in['pw_b'], 'L0_ffn_router_w': _L0_ffn_in['router_w'], 'L0_ffn_router_b': _L0_ffn_in['router_b'], 'L0_ffn_expert_w': _L0_ffn_in['expert_w'], 'L0_ffn_expert_b': _L0_ffn_in['expert_b'], 'L0_ffn_out_w': _L0_ffn_in['out_w'], 'L0_ffn_out_b': _L0_ffn_in['out_b'], 'L0_ffn_norm_w': _L0_ffn_in['norm_w'], 'L0_ffn_ff_down_w': _L0_ffn_in['ff_down_w'], 'L0_ffn_ff_down_b': _L0_ffn_in['ff_down_b'], 'L0_ffn_ff_up_w': _L0_ffn_in['ff_up_w'], 'L0_ffn_ff_up_b': _L0_ffn_in['ff_up_b']}

def reference(x, ctx_1024, mask_BxS2_bf1, mask_BxS2_bk0, L0_xattn_w_q, L0_xattn_w_k, L0_xattn_w_v, L0_xattn_w_out, L0_ffn_dw_kernel, L0_ffn_dw_bias, L0_ffn_pw_w, L0_ffn_pw_b, L0_ffn_router_w, L0_ffn_router_b, L0_ffn_expert_w, L0_ffn_expert_b, L0_ffn_out_w, L0_ffn_out_b, L0_ffn_norm_w, L0_ffn_ff_down_w, L0_ffn_ff_down_b, L0_ffn_ff_up_w, L0_ffn_ff_up_b):
    import jax
    import jax.numpy as jnp

    def _L0_xattn_ref(query, key_value, query_mask, kv_mask, w_q, w_k, w_v, w_out):
        import jax, jax.numpy as jnp
        import numpy as np
        D_MODEL = 256
        N_HEADS = 16
        NUM_KV_HEADS = 4
        D_K = D_MODEL // N_HEADS
        ROPE_BASE = 10000.0

        def _apply_rope(x, dim, base=ROPE_BASE, position_offset=0):
            T = x.shape[2]
            dtype = x.dtype
            theta = base ** (-jnp.arange(0, dim, 2, dtype=dtype) / dim)
            positions = jnp.arange(position_offset, position_offset + T, dtype=dtype)[:, None]
            angles = positions * theta[None, :]
            sin = jnp.sin(angles)[None, None]
            cos = jnp.cos(angles)[None, None]
            x1 = x[..., :dim // 2]
            x2 = x[..., dim // 2:dim]
            return jnp.concatenate([x1 * cos - x2 * sin, x1 * sin + x2 * cos], axis=-1)
        B, Tq, _ = query.shape
        Tkv = key_value.shape[1]
        group = N_HEADS // NUM_KV_HEADS
        Q = (query @ w_q).reshape(B, Tq, N_HEADS, D_K).transpose(0, 2, 1, 3)
        K = (key_value @ w_k).reshape(B, Tkv, NUM_KV_HEADS, D_K).transpose(0, 2, 1, 3)
        V = (key_value @ w_v).reshape(B, Tkv, NUM_KV_HEADS, D_K).transpose(0, 2, 1, 3)
        K = _apply_rope(K, D_K)
        Q = _apply_rope(Q, D_K)
        K = jnp.repeat(K, group, axis=1)
        V = jnp.repeat(V, group, axis=1)
        attn_mask = kv_mask[:, None, None, :] & query_mask[:, None, :, None]
        scale = 1.0 / jnp.sqrt(jnp.asarray(D_K, Q.dtype))
        scores = jnp.einsum('bhqd,bhkd->bhqk', Q, K) * scale
        scores = jnp.where(attn_mask, scores, jnp.finfo(scores.dtype).min)
        probs = jax.nn.softmax(scores, axis=-1)
        out = jnp.einsum('bhqk,bhkd->bhqd', probs, V)
        out = out.transpose(0, 2, 1, 3).reshape(B, Tq, D_MODEL)
        return out @ w_out

    def _L0_ffn_ref(x, dw_kernel, dw_bias, pw_w, pw_b, router_w, router_b, expert_w, expert_b, out_w, out_b, norm_w, ff_down_w, ff_down_b, ff_up_w, ff_up_b):
        import jax, jax.numpy as jnp
        import numpy as np
        from jax import lax
        B, L, D = (4, 512, 256)
        E, TOPK = (8, 2)
        K, DIL = (3, 1)
        HID = D // 4
        EPS = 1e-06

        def _rmsnorm(h, w):
            rms = jnp.sqrt(jnp.mean(h * h, axis=-1, keepdims=True) + EPS)
            return w * (h / rms)

        def _forward(x, dw_kernel, dw_bias, pw_w, pw_b, router_w, router_b, expert_w, expert_b, out_w, out_b, norm_w, ff_down_w, ff_down_b, ff_up_w, ff_up_b):
            pad = (K - 1) * DIL
            xc = jnp.transpose(x, (0, 2, 1))
            xc = lax.conv_general_dilated(xc, dw_kernel, window_strides=(1,), padding=((pad, 0),), rhs_dilation=(DIL,), dimension_numbers=('NCH', 'OIH', 'NCH'), feature_group_count=D) + dw_bias[None, :, None]
            xc = jax.nn.silu(jnp.einsum('bdl,ed->bel', xc, pw_w) + pw_b[None, :, None])
            x1 = x + jnp.transpose(xc, (0, 2, 1))
            logits = jnp.einsum('bsd,ed->bse', x1, router_w) + router_b
            top_v, top_i = lax.top_k(logits, TOPK)
            top_w = jax.nn.softmax(top_v, axis=-1)
            rw = jnp.sum(jax.nn.one_hot(top_i, E, dtype=x1.dtype) * top_w[..., None], axis=-2)
            ye = jax.nn.silu(jnp.einsum('bsd,eod->bseo', x1, expert_w) + expert_b)
            combined = jnp.einsum('bse,bseo->bso', rw, ye)
            moe_out = jnp.einsum('bsd,od->bso', combined, out_w) + out_b
            h = _rmsnorm(x1 + moe_out, norm_w)
            ff = jax.nn.gelu(jnp.einsum('bsd,hd->bsh', h, ff_down_w) + ff_down_b, approximate=False)
            ff = jnp.einsum('bsh,dh->bsd', ff, ff_up_w) + ff_up_b
            return h + ff
        return _forward(x, dw_kernel, dw_bias, pw_w, pw_b, router_w, router_b, expert_w, expert_b, out_w, out_b, norm_w, ff_down_w, ff_down_b, ff_up_w, ff_up_b)
    x = x + _L0_xattn_ref(_layernorm(x, axis=-1), ctx_1024, mask_BxS2_bf1, mask_BxS2_bk0, L0_xattn_w_q, L0_xattn_w_k, L0_xattn_w_v, L0_xattn_w_out)
    x = x + _L0_ffn_ref(_layernorm(x, axis=-1), L0_ffn_dw_kernel, L0_ffn_dw_bias, L0_ffn_pw_w, L0_ffn_pw_b, L0_ffn_router_w, L0_ffn_router_b, L0_ffn_expert_w, L0_ffn_expert_b, L0_ffn_out_w, L0_ffn_out_b, L0_ffn_norm_w, L0_ffn_ff_down_w, L0_ffn_ff_down_b, L0_ffn_ff_up_w, L0_ffn_ff_up_b)
    return x

_drawn_inputs = setup_inputs


def setup_inputs(seed=0):
    import zlib

    import numpy as np

    out = dict(_drawn_inputs(seed))
    spreads = {'L0_ffn_dw_bias': (0.0, 0.8),
     'L0_ffn_pw_b': (0.0, 0.305),
     'L0_ffn_router_b': (0.0, 0.8),
     'L0_ffn_expert_b': (0.0, 0.8),
     'L0_ffn_out_b': (0.0, 0.1),
     'L0_ffn_norm_w': (1.0, 0.2),
     'L0_ffn_ff_down_b': (0.0, 0.8),
     'L0_ffn_ff_up_b': (0.0, 0.1)}
    factors = {'L0_ffn_dw_kernel': 8.0,
     'L0_ffn_pw_w': 7.542,
     'L0_ffn_router_w': 3.643,
     'L0_ffn_expert_w': 3.184,
     'L0_ffn_out_w': 2.987,
     'L0_ffn_ff_down_w': 4.043,
     'L0_ffn_ff_up_w': 3.542}
    for name, (base, spread) in spreads.items():
        noise = np.random.default_rng([zlib.crc32(name.encode()), seed]).standard_normal(out[name].shape)
        drawn = base * np.exp(spread * noise) if base else spread * noise
        out[name] = jnp.asarray(drawn.astype(out[name].dtype))
    for name, factor in factors.items():
        out[name] = (out[name] * factor).astype(out[name].dtype)
    return out
```

```python
import math

import numpy as np

import concourse.bass as bass
from concourse import mybir
from contextlib import ExitStack

F32 = mybir.dt.float32
F32R = mybir.dt.float32r
BF16 = mybir.dt.bfloat16
U32 = mybir.dt.uint32
U8 = mybir.dt.uint8
ALU = mybir.AluOpType
ACT = mybir.ActivationFunctionType
AX = mybir.AxisListType

B, T, D = 16, 256, 256
NH, NG, DH = 16, 4, 16
R = NH // NG
P = 128
NT, NK = T // P, D // P
NE, TOPK = 8, 2
HID = D // 4
HALF = DH // 2
LN_EPS, RMS_EPS = 1e-5, 1e-6

Q_TERMS = (0, 0, 1, 1, 0, 2)
K_TERMS = (0, 1, 0, 1, 2, 0)
MASK_ROW = len(Q_TERMS) * DH
MAX_ROW = MASK_ROW + 1
S_ROWS = MASK_ROW + 1
ST_ROWS = MAX_ROW + 3
MASKED = -float(2.0 ** 100)

W_SIZES = (("q", NK * D), ("out", NK * D), ("pw", NK * D), ("router", NK * NE), ("moe_out", NK * D),
           ("down", NK * P), ("up", D), ("experts", NK * NE * D))
W_AT, _at = {}, 0
for _name, _size in W_SIZES:
    W_AT[_name] = (_at, _at + _size)
    _at += _size
W_COLS = _at
EARLY = W_AT["q"][1]

B_EXPERTS, B_MOE_OUT, B_UP, B_ROUTER = 0, NE * D, NE * D + D, NE * D + 2 * D
B_COLS = B_ROUTER + NE

WORK_COLS = 2 * NG * 2 * T + 2 * 2 * T + 9 * NT * D + 8 * D + T
CHUNKS = 8
Q_DMAS, K_DMAS = 2 * len(Q_TERMS) + 1, len(K_TERMS) + 1


def rope_tables():
    theta = np.float32(10000.0) ** (-np.arange(0, DH, 2, dtype=np.float32) / np.float32(DH))
    angle = (np.arange(T, dtype=np.float32)[:, None] * theta[None, :].astype(np.float32)).astype(np.float32)
    cos, sin = np.cos(angle).astype(np.float32).T, np.sin(angle).astype(np.float32).T
    scale = np.float32(1.0 / math.sqrt(DH))
    cq, sq = np.repeat(cos, NH, axis=0) * scale, np.repeat(sin, NH, axis=0) * scale
    ck, sk = np.repeat(cos, NG, axis=0), np.repeat(sin, NG, axis=0)
    q = np.stack([cq, cq, sq, -sq], axis=1)
    k = np.stack([np.concatenate([ck, ck]), np.concatenate([sk, -sk])], axis=1)
    return np.ascontiguousarray(q.astype(np.float32)), np.ascontiguousarray(k.astype(np.float32))


def build(nc, a, out):
    ctx = ExitStack()

    def sb(name, shape, dt=F32):
        return ctx.enter_context(nc.sbuf_tensor(name, shape, dt))[:]

    def ps(name, shape, dt=F32):
        return ctx.enter_context(nc.psum_tensor(name, shape, dt))[:]

    def sem(name):
        return ctx.enter_context(nc.semaphore(name))

    with ctx:
        work = sb("work", [P, WORK_COLS])
        carved = [0]

        def carve(*dims):
            n = math.prod(dims)
            view = work[:, carved[0]:carved[0] + n]
            carved[0] += n
            if len(dims) == 1:
                return view
            names = "a b c".split()[:len(dims)]
            return view.rearrange(f"p ({' '.join(names)}) -> p {' '.join(names)}",
                                  **dict(zip(names[1:], dims[1:])))

        w_late = work[:, 0:W_COLS - EARLY]
        bias_f = work[0:3, W_COLS - EARLY:W_COLS - EARLY + B_COLS]
        bias_t = work[0:3, W_COLS - EARLY + B_COLS:W_COLS - EARLY + B_COLS + B_COLS // 2].bitcast(BF16)
        masks_at = W_COLS - EARLY + B_COLS + B_COLS // 2
        key_m, qry_m, key_pen = (work[0:B, masks_at + n * T:masks_at + (n + 1) * T] for n in range(3))
        w_q = sb("w_q", [P, NK * D])
        w_hi = sb("w_hi", [P, W_COLS], F32R)
        w_lo = sb("w_lo", [P, W_COLS], F32R)
        wk = sb("wk", [P, NK, P])
        wv = sb("wv", [P, NK, NG * DH])
        ident = sb("ident", [P, P])
        ident_r = sb("ident_r", [P, P], F32R)
        ident_b = sb("ident_b", [P, P], BF16)
        ones_b = sb("ones_b", [P, P], BF16)
        ones_f = sb("ones_f", [P, P])
        bias_rows = sb("bias_rows", [P, B_COLS], BF16)
        conv_w = sb("conv_w", [P, NK, 3])
        conv_b = sb("conv_b", [P, NK])
        pw_b = sb("pw_b", [P, NK])
        down_b = sb("down_b", [P, 1])
        norm_w = sb("norm_w", [P, D])
        rope_q = sb("rope_q", [P, 4, T])
        rope_k = sb("rope_k", [2 * NG * HALF, 2, T])
        iota8 = sb("iota8", [P, NE])
        minus_half = sb("minus_half", [P, NT])
        key_m8 = sb("key_m8", [B, T], U8)
        qry_m8 = sb("qry_m8", [B, T], U8)
        tok_m8 = sb("tok_m8", [P, B * NT], U8)
        tok_m = sb("tok_m", [P, B, NT])
        any_key = sb("any_key", [B, 1])
        any_diag = sb("any_diag", [B, B])
        key_row = sb("key_row", [B, T], BF16)
        alive_row = sb("alive_row", [B, T], BF16)
        key_dram = nc.dram_tensor("key_rows", (B, T), BF16).ap()
        alive_dram = nc.dram_tensor("alive_rows", (B, T), BF16).ap()
        alive_tok = sb("alive_tok", [P, B, NT])
        xin = sb("xin", [P, 2, NT, D])
        ctxin = sb("ctxin", [P, 2, NK, T])
        st1 = sb("st1", [P, NT, 6])
        mv1 = sb("mv1", [P, NT, 2])
        ve1 = sb("ve1", [P, NT])
        pw1 = sb("pw1", [P, NT])
        rstd1 = sb("rstd1", [P, NT])
        xn = sb("xn", [P, NT, D])
        xT_hi = sb("xT_hi", [P, NK, T], F32R)
        xT_lo = sb("xT_lo", [P, NK, T], F32R)
        rq1 = sb("rq1", [P, 2, T])
        rq2 = sb("rq2", [P, 2, T])
        rk1 = sb("rk1", [64, T])
        rk2 = sb("rk2", [64, T])
        qk = sb("qk", [P, 3, T])
        qk_r = sb("qk_r", [P, 3, T])
        qk_t = [sb(f"qk_t{n}", [P, 3, T], BF16) for n in range(3)]
        q_stack = sb("q_stack", [P, 2, NH, T], BF16)
        k_stack = sb("k_stack", [P, 2, NG, T], BF16)
        v_aug = sb("v_aug", [P, 2, NT, NG, 32])
        mx = sb("mx", [P, NT, NH])
        mx_r = sb("mx_r", [P, NT, NH])
        mx_t = sb("mx_t", [P, NT, P], BF16)
        mT = sb("mT", [3 * NH, T], BF16)
        probs = carve(2, NG, 2 * T)
        o_sb = carve(2, 2 * T)
        rec = sb("rec", [P, NT, NH])
        on = carve(NT, D)
        onT_hi = sb("onT_hi", [P, NK, T], F32R)
        onT_lo = sb("onT_lo", [P, NK, T], F32R)
        xres = sb("xres", [P, NT, D])
        x1 = sb("x1", [P, 2, NT, D])
        st2 = sb("st2", [P, NT, 6])
        mv2 = sb("mv2", [P, NT, 2])
        ve2 = sb("ve2", [P, NT])
        rstd2 = sb("rstd2", [P, NT])
        xn2 = sb("xn2", [P, NT, D])
        z = sb("z", [P, NK, T + 2])
        cv = carve(NK, T)
        cv_hi = sb("cv_hi", [P, NK, T], F32R)
        cv_lo = sb("cv_lo", [P, NK, T], F32R)
        sp_ = carve(NK, T)
        u = carve(NK, T)
        u_hi = sb("u_hi", [P, 2, NK, T], F32R)
        u_lo = sb("u_lo", [P, 2, NK, T], F32R)
        top_v = sb("top_v", [P, NT, 8])
        top_i = sb("top_i", [P, NT, 8], U32)
        top_f = sb("top_f", [P, NT, TOPK])
        top_d = sb("top_d", [P, NT])
        top_th = sb("top_th", [P, NT])
        top_w = sb("top_w", [P, TOPK, NT])
        hot = sb("hot", [P, NT, 2, NE])
        rw = sb("rw", [P, 2, NT, NE])
        ys = carve(4, 2, D)
        acc = carve(NT, D)
        sq = carve(NT, D)
        ssum = sb("ssum", [P, NT])
        ms3 = sb("ms3", [P, NT])
        rstd3 = sb("rstd3", [P, NT])
        h = carve(NT, D)
        hx = carve(NT, D)
        hT_hi = sb("hT_hi", [P, NK, T], F32R)
        hT_lo = sb("hT_lo", [P, NK, T], F32R)
        cT_hi, cT_lo = hT_hi, hT_lo
        gl = carve(T)
        gl_hi = sb("gl_hi", [P, T], F32R)
        gl_lo = sb("gl_lo", [P, T], F32R)
        y = carve(NT, D)

        sc = [ps(f"sc{n}", [P, 1024]) for n in range(2)]
        e_bank = [ps(f"e{n}", [P, 512]) for n in range(2)]
        g_bank = [ps(f"g{n}", [P, 512]) for n in range(2)]

        names = """w_in wq_in wk_in small_in mask_in bias_in rope_in pool_const id_ready w_hi_ready w_lo_ready early_hi early_lo
            const_ready ident_cast bias_step mask_step mask_ready any_mm alive_ready mask_rows_out
            x_in0 x_in1 ctx_in0 ctx_in1 ln1_stats ln1_mv ln1_ve ln1_pow ln1_rstd xn_ready xT_mm xT_hi_ready xT_lo_ready kv_mm q_mm
            rope_q_step rope_k_step q_ready k_ready v_ready t0_ready r1_ready t1_ready t2_ready q_stack_in k_stack_in
            s_mm max_ready m_step m_ready mT_mm mT_ready m_rows_in st_mm exp_ready pv_mm o_ready oT_mm rec_ready on_ready
            onT_mm onT_hi_ready onT_lo_ready att_mm xres_in x1_ready
            ln2_stats ln2_mv ln2_ve ln2_rstd xn2_ready x2T_mm z_ready conv_step cv_hi_ready cv_lo_ready pw_mm sp_ready
            u_ready u_hi_ready u_lo_ready rt_mm topv_ready topi_ready topd_ready th_ready rw_step rw_ready
            ex_mm ys_ready comb_step cT_mm cT_hi_ready cT_lo_ready ow_mm sq_ready ms_ready rstd3_ready h_ready hx_ready
            hT_mm hT_hi_ready hT_lo_ready dn_mm gl_ready gl_hi_ready gl_lo_ready up_mm y_ready out_done dve_settled pool_settled""".split()
        S = {n: sem(n) for n in names}

        def wait(eng, name, value):
            if isinstance(value, int) and value <= 0:
                return
            eng.wait_ge(S[name], value)

        def settled(eng, name):
            eng.sem_inc(S[name], 1)

        def live(b):
            return not isinstance(b, int) or 0 <= b < B

        def pipeline(eng, body):
            for b in (-1, 0, 1, 2, 3):
                body(b, b % 2)
            with eng.Fori(4, B - 3, 2) as b:
                body(b, 0)
                body(b + 1, 1)
            for b in (B - 2, B - 1, B, B + 1):
                body(b, b % 2)

        def w(part, which):
            lo, hi = W_AT[which]
            return part[:, lo:hi]

        def w_late_k(which):
            lo, hi = W_AT[which]
            return w_late[:, lo - EARLY:hi - EARLY].rearrange("p (k n) -> p k n", k=NK)

        def w_k(part, which):
            return w(part, which).rearrange("p (k n) -> p k n", k=NK)

        up_late = w_late[:, W_AT["up"][0] - EARLY:W_AT["up"][1] - EARLY]
        block = ctx.enter_context(nc.Block())

        @block.sync
        def _(sp):
            def load(b, p):
                wait(sp, "xn_ready", 2 * (b - 1))
                sp.dma_start(xin[:, p], a["x_tok"][b]).then_inc(S[f"x_in{p}"], 16)
                wait(sp, "kv_mm", b - 1)
                sp.dma_start(ctxin[:, p], a["ctx_T"][b]).then_inc(S[f"ctx_in{p}"], 16)

            sp.dma_start(xin[:, 0], a["x_tok"][0]).then_inc(S["x_in0"], 16)
            sp.dma_start(tok_m8, a["qmask_tok"]).then_inc(S["mask_in"], 16)
            sp.dma_start(key_m8, a["key_mask"]).then_inc(S["mask_in"], 16)
            sp.dma_start(qry_m8, a["qry_mask"]).then_inc(S["mask_in"], 16)
            sp.dma_start(w_q.rearrange("p (k n) -> p k n", k=NK), a["w_q"]).then_inc(S["wq_in"], 16)
            sp.dma_start(ctxin[:, 0], a["ctx_T"][0]).then_inc(S["ctx_in0"], 16)
            sp.wait_ge(S["const_ready"], 1)
            sp.dma_start(wk[:, :, 0:NG * DH], a["w_k"]).then_inc(S["wk_in"], 16)
            sp.dma_start(wv, a["w_v"]).then_inc(S["wk_in"], 16)
            sp.dma_start(rope_q, a["rope_q"]).then_inc(S["rope_in"], 16)
            sp.dma_start(rope_k, a["rope_k"]).then_inc(S["rope_in"], 16)
            sp.dma_start(w_late_k("out"), a["w_out"]).then_inc(S["w_in"], 16)
            sp.dma_start(w_late_k("pw"), a["w_pw"]).then_inc(S["w_in"], 16)
            sp.dma_start(w_late_k("router"), a["w_router"]).then_inc(S["w_in"], 16)
            sp.dma_start(w_late_k("moe_out"), a["w_moe_out"]).then_inc(S["w_in"], 16)
            sp.dma_start(w_late_k("down")[:, :, 0:HID], a["w_down"]).then_inc(S["w_in"], 16)
            sp.dma_start(up_late[0:HID], a["w_up"]).then_inc(S["w_in"], 16)
            sp.dma_start(w_late_k("experts"), a["w_experts"]).then_inc(S["w_in"], 16)
            sp.dma_start(bias_f[:, B_EXPERTS:B_MOE_OUT], a["b_experts"].partition_broadcast(3)).then_inc(S["bias_in"], 16)
            sp.dma_start(bias_f[:, B_MOE_OUT:B_UP], a["b_moe_out"].partition_broadcast(3)).then_inc(S["bias_in"], 16)
            sp.dma_start(bias_f[:, B_UP:B_ROUTER], a["b_up"].partition_broadcast(3)).then_inc(S["bias_in"], 16)
            sp.dma_start(bias_f[:, B_ROUTER:B_COLS], a["b_router"].partition_broadcast(3)).then_inc(S["bias_in"], 16)
            sp.dma_start(conv_w, a["conv_w"]).then_inc(S["small_in"], 16)
            sp.dma_start(conv_b, a["conv_b"]).then_inc(S["small_in"], 16)
            sp.dma_start(pw_b, a["b_pw"]).then_inc(S["small_in"], 16)
            sp.dma_start(down_b[0:HID], a["b_down"]).then_inc(S["small_in"], 16)
            sp.dma_start(norm_w, a["norm_w"].partition_broadcast(P)).then_inc(S["small_in"], 16)
            sp.wait_ge(S["mask_ready"], 2)
            sp.dma_start(key_dram, key_row).then_inc(S["mask_rows_out"], 16)
            sp.dma_start(alive_dram, alive_row).then_inc(S["mask_rows_out"], 16)
            sp.wait_ge(S["mask_rows_out"], 32)
            sp.wait_ge(S["const_ready"], 10)

            def body(b, p):
                o = 1 - p
                if live(b + 2):
                    load(b + 2, p)
                if live(b):
                    wait(sp, "x1_ready", b)
                    sp.dma_start(xres, a["x_tok"][b]).then_inc(S["xres_in"], 16)
                    wait(sp, "mT_ready", b + 1)
                    sp.dma_start(q_stack[MAX_ROW:MAX_ROW + 3, p], mT).then_inc(S["m_rows_in"], 16)
                if live(b + 1):
                    n = b + 1
                    wait(sp, "st_mm", CHUNKS * b)
                    mask_q = alive_dram[bass.ds(n, 1)].unsqueeze(1).to_broadcast([1, NH, T])
                    mask_k = key_dram[bass.ds(n, 1)].unsqueeze(1).to_broadcast([1, NG, T])
                    sp.dma_start(q_stack[MASK_ROW:MASK_ROW + 1, o], mask_q).then_inc(S["q_stack_in"], 16)
                    sp.dma_start(k_stack[MASK_ROW:MASK_ROW + 1, o], mask_k).then_inc(S["k_stack_in"], 16)
                    for term, ready in ((0, "t0_ready"), (1, "t1_ready"), (2, "t2_ready")):
                        wait(sp, ready, n + 1)
                        for at, t in enumerate(K_TERMS):
                            if t == term:
                                sp.dma_start(k_stack[at * DH:(at + 1) * DH, o], qk_t[t][0:64, 2]).then_inc(S["k_stack_in"], 16)
                        for at, t in enumerate(Q_TERMS):
                            for half in range(2):
                                if t == term:
                                    row = at * DH + half * HALF
                                    sp.dma_start(q_stack[row:row + HALF, o], qk_t[t][:, half]).then_inc(S["q_stack_in"], 16)
                if live(b - 2):
                    wait(sp, "y_ready", b - 1)
                    sp.dma_start(out[b - 2], y).then_inc(S["out_done"], 16)

            pipeline(sp, body)
            sp.wait_ge(S["out_done"], 16 * B)

        @block.gpsimd
        def _(pool):
            g = nc.gpsimd
            g.memset(ident, 0.0).then_inc(S["pool_const"], 1)
            pool.wait_ge(S["pool_const"], 1)
            g.affine_select(out=ident, in_=ident, compare_op=ALU.not_equal, fill=1.0, base=0,
                            pattern=[[-1, P]], channel_multiplier=1).then_inc(S["id_ready"], 1)
            g.memset(minus_half, -0.5).then_inc(S["id_ready"], 1)
            g.iota(iota8, pattern=[[1, NE]], base=0, channel_multiplier=0,
                   allow_small_or_imprecise_dtypes=True).then_inc(S["id_ready"], 1)
            pool.wait_ge(S["id_ready"], 3)

            def body(b, p):
                o = 1 - p
                if live(b - 1):
                    wait(pool, "ln2_ve", b)
                    wait(pool, "xn2_ready", 2 * (b - 1))
                    g.tensor_tensor(rstd2, ve2, minus_half, ALU.pow).then_inc(S["ln2_rstd"], 1)
                if live(b + 1):
                    n = b + 1
                    wait(pool, "ln1_mv", 2 * n + 2)
                    wait(pool, "xn_ready", 2 * n)
                    settled(pool, "pool_settled")
                    g.tensor_scalar(ve1, mv1[:, :, 1], LN_EPS, 1.0, ALU.add, ALU.mult).then_inc(S["ln1_ve"], 1)
                    wait(pool, "ln1_ve", n + 1)
                    g.tensor_tensor(pw1, ve1, minus_half, ALU.pow).then_inc(S["ln1_pow"], 1)
                    if isinstance(n, int) and n == 0:
                        pool.wait_ge(S["alive_ready"], 1)
                    wait(pool, "ln1_pow", n + 1)
                    g.tensor_tensor(rstd1, pw1, alive_tok[:, bass.ds(n, 1)].rearrange("p o q -> p (o q)"),
                                    ALU.mult).then_inc(S["ln1_rstd"], 1)
                if live(b - 1):
                    m = b - 1
                    wait(pool, "cv_hi_ready", m + 1)
                    wait(pool, "pw_mm", m)
                    g.tensor_tensor(cv_lo, cv, cv_hi.bitcast(F32), ALU.subtract).then_inc(S["cv_lo_ready"], 1)
                    wait(pool, "topv_ready", 2 * m + 2)
                    g.tensor_tensor(top_d, top_v[:, :, 1], top_v[:, :, 0], ALU.subtract).then_inc(S["topd_ready"], 1)
                    wait(pool, "topi_ready", 2 * m + 2)
                    wait(pool, "rw_step", 7 * m)
                    settled(pool, "pool_settled")
                    g.tensor_copy(top_f, top_i[:, :, 0:TOPK]).then_inc(S["rw_step"], 1)
                    wait(pool, "th_ready", m + 1)
                    settled(pool, "pool_settled")
                    g.tensor_scalar(top_w[:, 0], top_th, -0.5, 0.5, ALU.mult, ALU.add).then_inc(S["rw_step"], 1)
                    g.tensor_scalar(top_w[:, 1], top_th, 0.5, 0.5, ALU.mult, ALU.add).then_inc(S["rw_step"], 1)
                    wait(pool, "rw_step", 7 * m + 3)
                    wait(pool, "rw_ready", 2 * m)
                    settled(pool, "pool_settled")
                    for q in range(NT):
                        for k in range(TOPK):
                            g.tensor_scalar(hot[:, q, k], iota8, top_f[:, q, k:k + 1], top_w[:, k, q:q + 1],
                                            ALU.is_equal, ALU.mult).then_inc(S["rw_step"], 1)
                    wait(pool, "rw_step", 7 * m + 7)
                    wait(pool, "comb_step", 16 * (m - 1))
                    for q in range(NT):
                        g.tensor_tensor(rw[:, o, q], hot[:, q, 0], hot[:, q, 1], ALU.add).then_inc(S["rw_ready"], 1)
                if live(b - 2):
                    m = b - 2
                    wait(pool, "sq_ready", 2 * m + 2)
                    settled(pool, "pool_settled")
                    g.tensor_scalar(ms3, ssum, 1.0 / D, RMS_EPS, ALU.mult, ALU.add).then_inc(S["ms_ready"], 1)
                    wait(pool, "ms_ready", m + 1)
                    wait(pool, "h_ready", 2 * m)
                    g.tensor_tensor(rstd3, ms3, minus_half, ALU.pow).then_inc(S["rstd3_ready"], 1)
                    wait(pool, "h_ready", 2 * m + 2)
                    wait(pool, "y_ready", m)
                    g.tensor_tensor(hx, h, x1[:, p], ALU.add).then_inc(S["hx_ready"], 1)
                if live(b + 1):
                    n = b + 1
                    wait(pool, "t0_ready", n + 1)
                    wait(pool, "t1_ready", n)
                    g.tensor_tensor(qk_r, qk, qk_t[0], ALU.subtract).then_inc(S["r1_ready"], 1)
                    wait(pool, "t1_ready", n + 1)
                    wait(pool, "q_stack_in", 16 * Q_DMAS * n)
                    wait(pool, "k_stack_in", 16 * K_DMAS * n)
                    g.tensor_tensor(qk_t[2], qk_r, qk_t[1], ALU.subtract).then_inc(S["t2_ready"], 1)
                if live(b - 2):
                    m = b - 2
                    wait(pool, "gl_hi_ready", m + 1)
                    wait(pool, "up_mm", m)
                    g.tensor_tensor(gl_lo, gl, gl_hi.bitcast(F32), ALU.subtract).then_inc(S["gl_lo_ready"], 1)

            pipeline(pool, body)

        @block.scalar
        def _(act):
            s = nc.scalar
            act.wait_ge(S["id_ready"], 1)
            s.activation(ident_r, ident, ACT.Copy).then_inc(S["ident_cast"], 1)
            s.activation(ident_b, ident, ACT.Copy).then_inc(S["ident_cast"], 1)
            act.wait_ge(S["wq_in"], 16)
            s.activation(w(w_hi, "q"), w_q, ACT.Copy).then_inc(S["early_hi"], 1)

            def ys_chunk(b, e):
                m = b - 2
                wait(act, "ex_mm", CHUNKS * m + e + 1)
                wait(act, "comb_step", 16 * m + max(0, 4 * ((e - 4) // 2) + 4))
                s.activation(ys[:, e % 4].rearrange("p a d -> p (a d)"), e_bank[e % 2],
                             ACT.Silu).then_inc(S["ys_ready"], 1)

            def exp_chunk(b, c):
                r = c // 2
                wait(act, "st_mm", CHUNKS * b + c + 1)
                wait(act, "pv_mm", 4 * b + r - 1)
                s.activation(probs[:, r % 2, 2 * (c % 2):2 * (c % 2) + 2].rearrange("p g n -> p (g n)"), sc[c % 2],
                             ACT.Exp).then_inc(S["exp_ready"], 1)

            def copy(dst, src, done):
                s.activation(dst, src, ACT.Copy).then_inc(S[done], 1)

            def flat(x):
                return x.rearrange("p k n -> p (k n)")

            def body(b, p):
                o = 1 - p
                A, Fr, M1, M2 = live(b), live(b + 1), live(b - 1), live(b - 2)
                m1, m2, n = b - 1, b - 2, b + 1
                if M2:
                    ys_chunk(b, 0)
                    ys_chunk(b, 1)
                if M1:
                    wait(act, "x2T_mm", m1 + 1)
                    wait(act, "u_ready", m1)
                    wait(act, "conv_step", 6 * m1)
                    s.activation(z[:, :, 2:T + 2], g_bank[0].rearrange("p (k n) -> p k n", k=NK),
                                 ACT.Copy).then_inc(S["z_ready"], 1)
                if M2:
                    ys_chunk(b, 2)
                    ys_chunk(b, 3)
                if M1:
                    wait(act, "conv_step", 6 * m1 + 6)
                    wait(act, "pw_mm", m1)
                    wait(act, "cv_lo_ready", m1)
                    copy(flat(cv_hi), flat(cv), "cv_hi_ready")
                if M2:
                    ys_chunk(b, 4)
                if M1:
                    if isinstance(b, int) and b == 1:
                        act.wait_ge(S["small_in"], 80)
                    wait(act, "pw_mm", m1 + 1)
                    for k in range(NK):
                        s.activation(sp_[:, k], g_bank[1][:, k * T:(k + 1) * T], ACT.Silu,
                                     bias=pw_b[:, k:k + 1]).then_inc(S["sp_ready"], 1)
                if M2:
                    ys_chunk(b, 5)
                if M1:
                    wait(act, "u_ready", m1 + 1)
                    wait(act, "ow_mm", m1 - 1)
                    copy(flat(u_hi[:, o]), flat(u), "u_hi_ready")
                if M2:
                    ys_chunk(b, 6)
                    ys_chunk(b, 7)
                if A:
                    wait(act, "mT_mm", b + 1)
                    wait(act, "m_rows_in", 16 * b)
                    copy(mT, g_bank[1].bitcast(BF16)[0:3 * NH, 0:T], "mT_ready")
                if M1:
                    wait(act, "topd_ready", m1 + 1)
                    wait(act, "rw_step", 7 * m1)
                    s.activation(top_th, top_d, ACT.Tanh, scale=0.5).then_inc(S["th_ready"], 1)
                if A:
                    if isinstance(b, int) and b == 0:
                        act.wait_ge(S["bias_step"], 9)
                    exp_chunk(b, 0)
                    exp_chunk(b, 1)
                if M2:
                    wait(act, "cT_mm", m2 + 1)
                    wait(act, "dn_mm", m2)
                    wait(act, "hT_lo_ready", m2)
                    copy(flat(cT_hi), e_bank[0], "cT_hi_ready")
                if Fr:
                    wait(act, "xT_mm", n + 1)
                    wait(act, "q_mm", n)
                    wait(act, "xT_lo_ready", n)
                    copy(flat(xT_hi), e_bank[1], "xT_hi_ready")
                if A:
                    exp_chunk(b, 2)
                    exp_chunk(b, 3)
                if M2:
                    wait(act, "ow_mm", m2 + 1)
                    wait(act, "ms_ready", m2)
                    wait(act, "sq_ready", 2 * m2)
                    for q in range(NT):
                        s.activation(sq[:, q], e_bank[1][:, q * D:(q + 1) * D], ACT.Square,
                                     accum_out=ssum[:, q:q + 1]).then_inc(S["sq_ready"], 1)
                if A:
                    exp_chunk(b, 4)
                    exp_chunk(b, 5)
                if Fr:
                    wait(act, "q_ready", n + 1)
                    wait(act, "k_ready", n + 1)
                    wait(act, "q_stack_in", 16 * Q_DMAS * n)
                    wait(act, "k_stack_in", 16 * K_DMAS * n)
                    copy(flat(qk_t[0]), flat(qk), "t0_ready")
                if A:
                    exp_chunk(b, 6)
                    exp_chunk(b, 7)
                if M2:
                    wait(act, "hT_mm", m2 + 1)
                    copy(flat(hT_hi), e_bank[1], "hT_hi_ready")
                if Fr:
                    wait(act, "r1_ready", n + 1)
                    wait(act, "t2_ready", n)
                    copy(flat(qk_t[1]), flat(qk_r), "t1_ready")
                if M2:
                    wait(act, "dn_mm", m2 + 1)
                    wait(act, "gl_lo_ready", m2)
                    s.activation(gl, e_bank[0][:, 0:T], ACT.Gelu, bias=down_b[:, 0:1]).then_inc(S["gl_ready"], 1)
                    wait(act, "gl_ready", m2 + 1)
                    wait(act, "up_mm", m2)
                    copy(gl_hi, gl, "gl_hi_ready")
                if A:
                    wait(act, "onT_mm", b + 1)
                    wait(act, "att_mm", b)
                    wait(act, "onT_lo_ready", b)
                    copy(flat(onT_hi), sc[1][:, 0:512], "onT_hi_ready")

            pipeline(act, body)

        @block.vector
        def _(dve):
            v = nc.vector
            v.memset(wk, 0.0).then_inc(S["const_ready"], 1)

            def link(ins, name, value):
                ins.then_inc(S[name], 1)
                dve.wait_ge(S[name], value)

            dve.wait_ge(S["mask_in"], 48)
            v.tensor_copy(key_m, key_m8).then_inc(S["mask_step"], 1)
            v.tensor_copy(qry_m, qry_m8).then_inc(S["mask_step"], 1)
            link(v.tensor_copy(tok_m.rearrange("p b q -> p (b q)"), tok_m8), "mask_step", 3)
            link(v.tensor_reduce(any_key, key_m, axis=AX.X, op=ALU.max), "mask_step", 4)
            link(v.tensor_scalar(key_pen, key_m, -1.0, -MASKED, ALU.add, ALU.mult), "mask_step", 5)
            v.tensor_scalar(key_row, key_pen, any_key, None, ALU.mult).then_inc(S["mask_ready"], 1)
            v.tensor_scalar(alive_row, qry_m, any_key, None, ALU.mult).then_inc(S["mask_ready"], 1)
            v.memset(ones_f, 1.0).then_inc(S["mask_step"], 1)
            dve.wait_ge(S["id_ready"], 1)
            link(v.tensor_scalar(any_diag, ident[0:B, 0:B], any_key, None, ALU.mult), "mask_step", 7)
            dve.wait_ge(S["any_mm"], 1)
            v.tensor_tensor(alive_tok, tok_m, e_bank[0][:, 0:B].unsqueeze(2).to_broadcast([P, B, NT]),
                            ALU.mult).then_inc(S["alive_ready"], 1)
            v.memset(ones_b, 1.0).then_inc(S["const_ready"], 1)
            v.memset(bias_rows, 0.0).then_inc(S["bias_step"], 1)
            v.memset(down_b[HID:P], 0.0).then_inc(S["const_ready"], 1)
            v.memset(w_late_k("down")[:, :, HID:P], 0.0).then_inc(S["const_ready"], 1)
            v.memset(up_late[HID:P], 0.0).then_inc(S["const_ready"], 1)
            v.memset(qk, 0.0).then_inc(S["const_ready"], 1)
            v.memset(mx_t, 0.0).then_inc(S["const_ready"], 1)
            v.memset(z, 0.0).then_inc(S["const_ready"], 1)
            v.memset(k_stack[MASK_ROW:ST_ROWS], 1.0).then_inc(S["const_ready"], 1)
            v.memset(v_aug, 0.0).then_inc(S["const_ready"], 1)
            dve.wait_ge(S["const_ready"], 10)
            v.memset(v_aug[:, :, :, :, DH:DH + 1], 1.0).then_inc(S["const_ready"], 1)
            dve.wait_ge(S["const_ready"], 11)
            dve.wait_ge(S["early_hi"], 1)
            v.tensor_tensor(w(w_lo, "q"), w_q, w(w_hi, "q").bitcast(F32), ALU.subtract).then_inc(S["early_lo"], 1)

            def late_weights():
                dve.wait_ge(S["small_in"], 80)
                dve.wait_ge(S["w_in"], 16 * (len(W_SIZES) - 1))
                v.tensor_copy(w_hi[:, EARLY:], w_late).then_inc(S["w_hi_ready"], 1)
                dve.wait_ge(S["w_hi_ready"], 1)
                v.tensor_tensor(w_lo[:, EARLY:], w_late, w_hi[:, EARLY:].bitcast(F32),
                                ALU.subtract).then_inc(S["w_lo_ready"], 1)
                dve.wait_ge(S["bias_in"], 64)
                for n in range(3):
                    link(v.tensor_copy(bias_t, bias_f), "bias_step", 3 * n + 2)
                    if n < 2:
                        link(v.tensor_tensor(bias_f, bias_f, bias_t, ALU.subtract), "bias_step", 3 * n + 3)
                    link(v.scalar_tensor_tensor(bias_rows[0:3], bias_t, ident[0:3, n:n + 1], bias_rows[0:3],
                                                ALU.mult, ALU.add), "bias_step", 3 * n + 4 if n < 2 else 9)

            def flat(x):
                return x.rearrange("p k n -> p (k n)")

            def lo_part(dst, src, hi, hi_ready, n, done):
                dve.wait_ge(S[hi_ready], n + 1)
                v.tensor_tensor(flat(dst), src, flat(hi).bitcast(F32), ALU.subtract).then_inc(S[done], 1)

            def maxima(b, c):
                q, g = c // NG, c % NG
                wait(dve, "s_mm", CHUNKS * b + c + 1)
                if c == 0:
                    wait(dve, "m_step", 3 * b)
                    wait(dve, "m_ready", b)
                v.tensor_reduce(mx[:, q, R * g:R * g + R], sc[c % 2].rearrange("p (r n) -> p r n", r=R),
                                axis=AX.X, op=ALU.max).then_inc(S["max_ready"], 1)

            def combine(b, p, pair):
                m = b - 2
                wait(dve, "ys_ready", CHUNKS * m + 2 * pair + 2)
                if pair == 0:
                    wait(dve, "rw_ready", 2 * m + 2)
                    wait(dve, "cT_mm", m)
                for k in range(2):
                    for q in range(NT):
                        done = 16 * m + 4 * pair + 2 * k + q
                        src = ys[:, (2 * pair + q) % 4, k]
                        weight = rw[:, p, q, 2 * pair + k:2 * pair + k + 1]
                        if pair == 0 and k == 0:
                            v.tensor_scalar(acc[:, q], src, weight, None, ALU.mult).then_inc(S["comb_step"], 1)
                        else:
                            wait(dve, "comb_step", done - 1)
                            v.scalar_tensor_tensor(acc[:, q], src, weight, acc[:, q], ALU.mult,
                                                   ALU.add).then_inc(S["comb_step"], 1)

            def body(b, p):
                o = 1 - p
                A, Fr, M1, M2 = live(b), live(b + 1), live(b - 1), live(b - 2)
                m1, m2, n = b - 1, b - 2, b + 1
                if M1:
                    wait(dve, "x1_ready", m1 + 1)
                    wait(dve, "ln2_mv", 2 * m1)
                    for q in range(NT):
                        v.bn_stats(st2[:, q], x1[:, o, q]).then_inc(S["ln2_stats"], 1)
                    wait(dve, "ln2_stats", 2 * m1 + 2)
                    wait(dve, "ln2_ve", m1)
                    wait(dve, "xn2_ready", 2 * m1)
                    settled(dve, "dve_settled")
                    for q in range(NT):
                        v.bn_aggr(mv2[:, q], st2[:, q]).then_inc(S["ln2_mv"], 1)
                    wait(dve, "ln2_mv", 2 * m1 + 2)
                    wait(dve, "ln2_rstd", m1)
                    v.tensor_scalar(ve2, mv2[:, :, 1], LN_EPS, None, ALU.add).then_inc(S["ln2_ve"], 1)
                if Fr:
                    wait(dve, f"x_in{o}", 8 * (n - o) + 16)
                    wait(dve, "ln1_mv", 2 * n)
                    for q in range(NT):
                        v.bn_stats(st1[:, q], xin[:, o, q]).then_inc(S["ln1_stats"], 1)
                    wait(dve, "ln1_stats", 2 * n + 2)
                    wait(dve, "ln1_ve", n)
                    wait(dve, "xn_ready", 2 * n)
                    settled(dve, "dve_settled")
                    for q in range(NT):
                        v.bn_aggr(mv1[:, q], st1[:, q]).then_inc(S["ln1_mv"], 1)
                if A:
                    maxima(b, 0)
                if M1:
                    wait(dve, "ln2_rstd", m1 + 1)
                    wait(dve, "x2T_mm", m1)
                    for q in range(NT):
                        v.tensor_scalar(xn2[:, q], x1[:, o, q], mv2[:, q, 0:1], rstd2[:, q:q + 1], ALU.subtract,
                                        ALU.mult).then_inc(S["xn2_ready"], 1)
                if A:
                    maxima(b, 1)
                if M2:
                    combine(b, p, 0)
                if Fr:
                    wait(dve, "ln1_mv", 2 * n + 2)
                    wait(dve, "ln1_rstd", n + 1)
                    wait(dve, "xT_mm", n)
                    for q in range(NT):
                        v.tensor_scalar(xn[:, q], xin[:, o, q], mv1[:, q, 0:1], rstd1[:, q:q + 1], ALU.subtract,
                                        ALU.mult).then_inc(S["xn_ready"], 1)
                if A:
                    maxima(b, 2)
                if M1:
                    wait(dve, "z_ready", m1 + 1)
                    wait(dve, "cv_hi_ready", m1)
                    wait(dve, "cv_lo_ready", m1)
                    for k in range(NK):
                        v.tensor_scalar(cv[:, k], z[:, k, 2:T + 2], conv_w[:, k, 2:3], conv_b[:, k:k + 1], ALU.mult,
                                        ALU.add).then_inc(S["conv_step"], 1)
                    for tap in (1, 0):
                        for k in range(NK):
                            wait(dve, "conv_step", 6 * m1 + 2 * (2 - tap) + k - 1)
                            v.scalar_tensor_tensor(cv[:, k], z[:, k, tap:T + tap], conv_w[:, k, tap:tap + 1], cv[:, k],
                                                   ALU.mult, ALU.add).then_inc(S["conv_step"], 1)
                if A:
                    maxima(b, 3)
                if M2:
                    combine(b, p, 1)
                if A:
                    maxima(b, 4)
                if M1:
                    wait(dve, "sp_ready", 2 * m1 + 2)
                    wait(dve, "u_hi_ready", m1)
                    wait(dve, "u_lo_ready", m1)
                    v.tensor_tensor(u, z[:, :, 2:T + 2], sp_, ALU.add).then_inc(S["u_ready"], 1)
                if A:
                    maxima(b, 5)
                if M2:
                    combine(b, p, 2)
                if M1:
                    wait(dve, "u_ready", m1 + 1)
                    lo_part(u_lo[:, o], flat(u), u_hi[:, o], "u_hi_ready", m1, "u_lo_ready")
                if A:
                    maxima(b, 6)
                    maxima(b, 7)
                    wait(dve, "max_ready", CHUNKS * (b + 1))
                    wait(dve, "mT_mm", b)
                    link(v.tensor_scalar(mx_t[:, :, 0:NH], mx, -1.0, None, ALU.mult), "m_step", 3 * b + 1)
                    link(v.scalar_tensor_tensor(mx_r, mx, -1.0, mx_t[:, :, 0:NH], ALU.mult, ALU.subtract),
                         "m_step", 3 * b + 2)
                    link(v.tensor_copy(mx_t[:, :, NH:2 * NH], mx_r), "m_step", 3 * b + 3)
                    v.tensor_tensor(mx_t[:, :, 2 * NH:3 * NH], mx_r, mx_t[:, :, NH:2 * NH],
                                    ALU.subtract).then_inc(S["m_ready"], 1)
                if M2:
                    combine(b, p, 3)
                if M1:
                    wait(dve, "rt_mm", m1 + 1)
                    wait(dve, "topd_ready", m1)
                    settled(dve, "dve_settled")
                    for q in range(NT):
                        v.max(top_v[:, q], g_bank[0][:, q * NE:(q + 1) * NE]).then_inc(S["topv_ready"], 1)
                    wait(dve, "topv_ready", 2 * m1 + 2)
                    wait(dve, "rw_step", 7 * m1)
                    settled(dve, "dve_settled")
                    for q in range(NT):
                        v.max_index(top_i[:, q], top_v[:, q], g_bank[0][:, q * NE:(q + 1) * NE]).then_inc(S["topi_ready"], 1)
                if M2:
                    wait(dve, "dn_mm", m2)
                    lo_part(cT_lo, e_bank[0], cT_hi, "cT_hi_ready", m2, "cT_lo_ready")
                if Fr:
                    wait(dve, "q_mm", n)
                    lo_part(xT_lo, e_bank[1], xT_hi, "xT_hi_ready", n, "xT_lo_ready")
                    if isinstance(n, int) and n == 0:
                        dve.wait_ge(S["rope_in"], 32)
                    wait(dve, "kv_mm", n + 1)
                    wait(dve, "k_ready", n)
                    ks = e_bank[0]
                    v.tensor_tensor(rk1, ks[0:64, 0:T], rope_k[:, 0], ALU.mult).then_inc(S["rope_k_step"], 1)
                    v.tensor_tensor(rk2[32:64], ks[0:32, 0:T], rope_k[0:32, 1], ALU.mult).then_inc(S["rope_k_step"], 1)
                    v.tensor_tensor(rk2[0:32], ks[32:64, 0:T], rope_k[32:64, 1], ALU.mult).then_inc(S["rope_k_step"], 1)
                    wait(dve, "pv_mm", 4 * (n - 1))
                    v.tensor_copy(v_aug[:, o, :, :, 0:DH],
                                  ks[:, T:T + NT * NG * DH].rearrange("p (t g d) -> p t g d", t=NT, g=NG)).then_inc(S["v_ready"], 1)
                    wait(dve, "rope_k_step", 3 * n + 3)
                    wait(dve, "t0_ready", n)
                    wait(dve, "r1_ready", n)
                    v.tensor_tensor(qk[0:64, 2], rk1, rk2, ALU.add).then_inc(S["k_ready"], 1)
                if M2:
                    wait(dve, "rstd3_ready", m2 + 1)
                    wait(dve, "hT_mm", m2)
                    wait(dve, "hx_ready", m2)
                    for q in range(NT):
                        v.scalar_tensor_tensor(h[:, q], e_bank[1][:, q * D:(q + 1) * D], rstd3[:, q:q + 1], norm_w,
                                               ALU.mult, ALU.mult).then_inc(S["h_ready"], 1)
                if A:
                    wait(dve, "pv_mm", 4 * b + 2)
                    wait(dve, "oT_mm", 2 * b)
                    v.tensor_copy(o_sb[:, 0], g_bank[0]).then_inc(S["o_ready"], 1)
                if Fr:
                    wait(dve, "q_mm", n + 1)
                    wait(dve, "q_ready", n)
                    qs = e_bank[0]
                    v.tensor_tensor(flat(rq1), qs, flat(rope_q[:, 0:2]), ALU.mult).then_inc(S["rope_q_step"], 1)
                    v.tensor_tensor(rq2[:, 1], qs[:, 0:T], rope_q[:, 2], ALU.mult).then_inc(S["rope_q_step"], 1)
                    v.tensor_tensor(rq2[:, 0], qs[:, T:2 * T], rope_q[:, 3], ALU.mult).then_inc(S["rope_q_step"], 1)
                    wait(dve, "rope_q_step", 3 * n + 3)
                    v.tensor_tensor(qk[:, 0:2], rq1, rq2, ALU.add).then_inc(S["q_ready"], 1)
                if M2:
                    wait(dve, "ow_mm", m2 + 1)
                    lo_part(hT_lo, e_bank[1], hT_hi, "hT_hi_ready", m2, "hT_lo_ready")
                if A:
                    wait(dve, "pv_mm", 4 * b + 4)
                    v.tensor_copy(o_sb[:, 1], g_bank[1]).then_inc(S["o_ready"], 1)
                    wait(dve, "oT_mm", 2 * b + 2)
                    wait(dve, "on_ready", 2 * b)
                    wait(dve, "onT_mm", b)
                    oq = [sc[0][:, q * 512:(q + 1) * 512].rearrange("p (r g d) -> p r g d", r=R, g=NG) for q in range(NT)]
                    for q in range(NT):
                        v.reciprocal(rec[:, q].rearrange("p (r g) -> p r g", r=R), oq[q][:, :, :, DH]).then_inc(S["rec_ready"], 1)
                    for q in range(NT):
                        wait(dve, "rec_ready", 2 * b + q + 1)
                        v.tensor_tensor(on[:, q].rearrange("p (g r d) -> p r g d", g=NG, r=R), oq[q][:, :, :, 0:DH],
                                        rec[:, q].rearrange("p (r g) -> p r g", r=R).unsqueeze(3).to_broadcast([P, R, NG, DH]),
                                        ALU.mult).then_inc(S["on_ready"], 1)
                    wait(dve, "att_mm", b)
                    lo_part(onT_lo, sc[1][:, 0:512], onT_hi, "onT_hi_ready", b, "onT_lo_ready")
                    wait(dve, "att_mm", b + 1)
                    wait(dve, "xres_in", 16 * (b + 1))
                    wait(dve, "hx_ready", b - 1)
                    wait(dve, "xn2_ready", 2 * (b - 1))
                    v.tensor_tensor(flat(x1[:, p]), sc[1][:, 512:1024], flat(xres), ALU.add).then_inc(S["x1_ready"], 1)
                if M2:
                    wait(dve, "up_mm", m2 + 1)
                    wait(dve, "hx_ready", m2 + 1)
                    wait(dve, "out_done", 16 * m2)
                    v.tensor_tensor(flat(y), e_bank[0], flat(hx), ALU.add).then_inc(S["y_ready"], 1)
                if isinstance(b, int) and b == -1:
                    late_weights()

            pipeline(dve, body)

        @block.tensor
        def _(pe):
            t = nc.tensor
            pe.wait_ge(S["mask_step"], 7)
            t.matmul(e_bank[0][:, 0:B], ones_f[0:B, :], any_diag, start=True, stop=True).then_inc(S["any_mm"], 1)
            pe.wait_ge(S["const_ready"], 11)
            pe.wait_ge(S["ident_cast"], 2)
            pe.wait_ge(S["id_ready"], 1)
            pe.wait_ge(S["alive_ready"], 1)

            def mm3(dst, l_hi, l_lo, r_hi, r_lo, start, stop):
                t.matmul(dst, l_hi, r_hi, start=start, stop=False)
                t.matmul(dst, l_hi, r_lo, start=False, stop=False)
                return t.matmul(dst, l_lo, r_hi, start=False, stop=stop)

            def bias(dst, at, n, stop=True):
                return t.matmul(dst, ones_b, bias_rows[:, at:at + n], start=False, stop=stop)

            def transposes(dst, src, done):
                for k in range(NK):
                    for q in range(NT):
                        last = t.transpose(dst[:, k * T + q * P:k * T + (q + 1) * P], src[:, q, k * P:(k + 1) * P], ident)
                last.then_inc(S[done], 1)

            def token_major(dst, l_hi, l_lo, which, q):
                for k in range(NK):
                    last = mm3(dst, l_hi[:, k, q * P:(q + 1) * P], l_lo[:, k, q * P:(q + 1) * P],
                               w_k(w_hi, which)[:, k], w_k(w_lo, which)[:, k], k == 0, k == NK - 1)
                return last

            def scores(b, p, c):
                q, g = c // NG, c % NG
                if c >= 2:
                    wait(pe, "max_ready", CHUNKS * b + c - 1)
                elif c == 0:
                    wait(pe, "x1_ready", b)
                    wait(pe, "q_stack_in", 16 * Q_DMAS * (b + 1))
                    wait(pe, "k_stack_in", 16 * K_DMAS * (b + 1))
                for r in range(R):
                    last = t.matmul(sc[c % 2][:, r * T:(r + 1) * T],
                                    q_stack[0:S_ROWS, p, R * g + r, q * P:(q + 1) * P],
                                    k_stack[0:S_ROWS, p, g], start=True, stop=True)
                last.then_inc(S["s_mm"], 1)

            def scores_T(b, p, r):
                half, kt = r // 2, r % 2
                for j in range(2):
                    c = 2 * r + j
                    if c == 0:
                        wait(pe, "m_rows_in", 16 * (b + 1))
                    elif c >= 2:
                        wait(pe, "exp_ready", CHUNKS * b + c - 1)
                    for i in range(2):
                        g = 2 * j + i
                        last = t.matmul(sc[c % 2][:, i * 512:(i + 1) * 512],
                                        k_stack[0:ST_ROWS, p, g, kt * P:(kt + 1) * P],
                                        q_stack[0:ST_ROWS, p, R * g + 2 * half:R * g + 2 * half + 2],
                                        start=True, stop=True)
                    last.then_inc(S["st_mm"], 1)

            def values(b, p, r):
                half, kt = r // 2, r % 2
                wait(pe, "exp_ready", CHUNKS * b + 2 * r + 2)
                if r == 0:
                    wait(pe, "topi_ready", 2 * b)
                for g in range(NG):
                    last = t.matmul(g_bank[half][32 * g:32 * g + 32], v_aug[:, p, kt, g], probs[:, r % 2, g],
                                    start=(kt == 0), stop=(kt == NT - 1))
                last.then_inc(S["pv_mm"], 1)

            def experts(b, p, e):
                m = b - 2
                q, ec = e % 2, e // 2
                if e == 0:
                    wait(pe, "y_ready", m)
                    if live(b):
                        wait(pe, "rope_q_step", 3 * b + 3)
                elif e == 1:
                    wait(pe, "hT_lo_ready", m)
                    if live(b):
                        wait(pe, "xT_lo_ready", b + 1)
                else:
                    wait(pe, "ys_ready", CHUNKS * m + e - 1)
                for k in range(NK):
                    at = slice(ec * 512, (ec + 1) * 512)
                    mm3(e_bank[e % 2], u_hi[:, p, k, q * P:(q + 1) * P], u_lo[:, p, k, q * P:(q + 1) * P],
                        w_k(w_hi, "experts")[:, k, at], w_k(w_lo, "experts")[:, k, at], k == 0, False)
                bias(e_bank[e % 2], B_EXPERTS + ec * 512, 512).then_inc(S["ex_mm"], 1)

            def body(b, p):
                o = 1 - p
                A, Fr, M1, M2 = live(b), live(b + 1), live(b - 1), live(b - 2)
                m1, m2, n = b - 1, b - 2, b + 1
                if M2:
                    experts(b, p, 0)
                    experts(b, p, 1)
                if A:
                    scores(b, p, 0)
                    scores(b, p, 1)
                if M1:
                    wait(pe, "xn2_ready", 2 * m1 + 2)
                    wait(pe, "topi_ready", 2 * m1)
                    wait(pe, "o_ready", 2 * m1 + 2)
                    transposes(g_bank[0], xn2, "x2T_mm")
                if M2:
                    experts(b, p, 2)
                if A:
                    scores(b, p, 2)
                if M2:
                    experts(b, p, 3)
                if A:
                    scores(b, p, 3)
                if M1:
                    if isinstance(b, int) and b == 1:
                        pe.wait_ge(S["w_lo_ready"], 1)
                        pe.wait_ge(S["bias_step"], 9)
                    wait(pe, "cv_lo_ready", m1 + 1)
                    for half in range(NK):
                        for k in range(NK):
                            at = slice(half * P, (half + 1) * P)
                            last = mm3(g_bank[1][:, half * T:(half + 1) * T], w_k(w_hi, "pw")[:, k, at],
                                       w_k(w_lo, "pw")[:, k, at], cv_hi[:, k], cv_lo[:, k], k == 0, k == NK - 1)
                    last.then_inc(S["pw_mm"], 1)
                if M2:
                    experts(b, p, 4)
                if A:
                    scores(b, p, 4)
                if M2:
                    experts(b, p, 5)
                if A:
                    scores(b, p, 5)
                if M2:
                    experts(b, p, 6)
                if A:
                    scores(b, p, 6)
                    scores(b, p, 7)
                if M2:
                    experts(b, p, 7)
                if M1:
                    wait(pe, "u_lo_ready", m1 + 1)
                    for q in range(NT):
                        at = g_bank[0][:, q * NE:(q + 1) * NE]
                        token_major_router = [mm3(at, u_hi[:, o, k, q * P:(q + 1) * P], u_lo[:, o, k, q * P:(q + 1) * P],
                                                  w_k(w_hi, "router")[:, k], w_k(w_lo, "router")[:, k], k == 0, False)
                                              for k in range(NK)]
                        last = bias(at, B_ROUTER, NE)
                    last.then_inc(S["rt_mm"], 1)
                if A:
                    wait(pe, "m_ready", b + 1)
                    wait(pe, "sp_ready", 2 * b)
                    for q in range(NT):
                        last = t.transpose(g_bank[1].bitcast(BF16)[:, q * P:(q + 1) * P], mx_t[:, q], ident_b)
                    last.then_inc(S["mT_mm"], 1)
                    scores_T(b, p, 0)
                if M2:
                    wait(pe, "comb_step", 16 * m2 + 16)
                    wait(pe, "ys_ready", CHUNKS * m2 + 8)
                    transposes(e_bank[0], acc, "cT_mm")
                if Fr:
                    wait(pe, "xn_ready", 2 * n + 2)
                    transposes(e_bank[1], xn, "xT_mm")
                if A:
                    scores_T(b, p, 1)
                    values(b, p, 0)
                if M2:
                    wait(pe, "cT_lo_ready", m2 + 1)
                    if Fr:
                        wait(pe, "xT_lo_ready", n + 1)
                    for q in range(NT):
                        at = e_bank[1][:, q * D:(q + 1) * D]
                        for k in range(NK):
                            mm3(at, cT_hi[:, k, q * P:(q + 1) * P], cT_lo[:, k, q * P:(q + 1) * P],
                                w_k(w_hi, "moe_out")[:, k], w_k(w_lo, "moe_out")[:, k], k == 0, False)
                        for k in range(NK):
                            for part in (u_hi, u_lo):
                                t.matmul(at[:, k * P:(k + 1) * P], part[:, p, k, q * P:(q + 1) * P], ident_r,
                                         start=False, stop=False)
                        last = bias(at, B_MOE_OUT, D)
                    last.then_inc(S["ow_mm"], 1)
                if Fr:
                    wait(pe, f"ctx_in{o}", 8 * (n - o) + 16)
                    if isinstance(n, int) and n == 0:
                        pe.wait_ge(S["wk_in"], 32)
                    if M2:
                        wait(pe, "cT_lo_ready", m2 + 1)
                    for k in range(NK):
                        t.matmul(e_bank[0][:, 0:T], wk[:, k], ctxin[:, o, k], start=(k == 0), stop=(k == NK - 1))
                    for kt in range(NT):
                        at = e_bank[0][:, T + kt * 64:T + (kt + 1) * 64]
                        for k in range(NK):
                            last = t.matmul(at, ctxin[:, o, k, kt * P:(kt + 1) * P], wv[:, k], start=(k == 0),
                                            stop=(k == NK - 1))
                    last.then_inc(S["kv_mm"], 1)
                if A:
                    scores_T(b, p, 2)
                    values(b, p, 1)
                if Fr:
                    wait(pe, "xT_lo_ready", n + 1)
                    wait(pe, "rope_k_step", 3 * n + 3)
                    wait(pe, "v_ready", n + 1)
                    if isinstance(n, int) and n == 0:
                        pe.wait_ge(S["early_lo"], 1)
                    for half in range(2):
                        for k in range(NK):
                            at = slice(half * P, (half + 1) * P)
                            last = mm3(e_bank[0][:, half * T:(half + 1) * T], w_k(w_hi, "q")[:, k, at],
                                       w_k(w_lo, "q")[:, k, at], xT_hi[:, k], xT_lo[:, k], k == 0, k == NK - 1)
                    last.then_inc(S["q_mm"], 1)
                if A:
                    scores_T(b, p, 3)
                    values(b, p, 2)
                if M2:
                    wait(pe, "h_ready", 2 * m2 + 2)
                    transposes(e_bank[1], h, "hT_mm")
                if A:
                    values(b, p, 3)
                    wait(pe, "o_ready", 2 * b + 2)
                    wait(pe, "exp_ready", CHUNKS * b + 8)
                    for q in range(NT):
                        for r in range(R):
                            last = t.transpose(sc[0][:, q * 512 + r * P:q * 512 + (r + 1) * P],
                                               o_sb[:, r // 2, (r % 2) * T + q * P:(r % 2) * T + (q + 1) * P], ident)
                        last.then_inc(S["oT_mm"], 1)
                if M2:
                    wait(pe, "hT_lo_ready", m2 + 1)
                    if Fr:
                        wait(pe, "rope_q_step", 3 * n + 3)
                    for k in range(NK):
                        last = mm3(e_bank[0][:, 0:T], w_k(w_hi, "down")[:, k], w_k(w_lo, "down")[:, k], hT_hi[:, k],
                                   hT_lo[:, k], k == 0, k == NK - 1)
                    last.then_inc(S["dn_mm"], 1)
                if A:
                    wait(pe, "on_ready", 2 * b + 2)
                    transposes(sc[1][:, 0:512], on, "onT_mm")
                    wait(pe, "onT_lo_ready", b + 1)
                    for q in range(NT):
                        last = token_major(sc[1][:, 512 + q * D:512 + (q + 1) * D], onT_hi, onT_lo, "out", q)
                    last.then_inc(S["att_mm"], 1)
                if M2:
                    wait(pe, "gl_lo_ready", m2 + 1)
                    wait(pe, "gl_ready", m2 + 1)
                    for q in range(NT):
                        at = e_bank[0][:, q * D:(q + 1) * D]
                        mm3(at, gl_hi[:, q * P:(q + 1) * P], gl_lo[:, q * P:(q + 1) * P], w(w_hi, "up"), w(w_lo, "up"),
                            True, False)
                        last = bias(at, B_UP, D)
                    last.then_inc(S["up_mm"], 1)

            pipeline(pe, body)


def layouts(i):
    f = lambda x: np.ascontiguousarray(x)
    x = np.asarray(i["x"])
    feat = lambda wt: f(wt.reshape(NK, P, -1).transpose(1, 0, 2))
    col = lambda v: f(v.reshape(NK, P).T)
    w_q = np.asarray(i["L0_xattn_w_q"]).reshape(D, NH, 2, HALF).transpose(0, 2, 3, 1).reshape(D, D)
    w_k = np.asarray(i["L0_xattn_w_k"]).reshape(D, NG, 2, HALF).transpose(0, 2, 3, 1).reshape(D, NG * DH)
    rope_q, rope_k = rope_tables()
    key_mask = np.asarray(i["mask_BxS2_bk0"])
    qry_mask = np.asarray(i["mask_BxS2_bf1"])
    return {
        "x_tok": f(x.reshape(B, NT, P, D).transpose(0, 2, 1, 3)),
        "ctx_T": f(np.asarray(i["ctx_1024"]).transpose(0, 2, 1).reshape(B, NK, P, T).transpose(0, 2, 1, 3)),
        "key_mask": f(key_mask),
        "qry_mask": f(qry_mask),
        "qmask_tok": f(qry_mask.reshape(B, NT, P).transpose(2, 0, 1).reshape(P, B * NT)),
        "w_q": feat(w_q),
        "w_k": feat(w_k),
        "w_v": feat(np.asarray(i["L0_xattn_w_v"])),
        "w_out": feat(np.asarray(i["L0_xattn_w_out"])),
        "w_pw": feat(np.asarray(i["L0_ffn_pw_w"]).T),
        "w_router": feat(np.asarray(i["L0_ffn_router_w"]).T),
        "w_moe_out": feat(np.asarray(i["L0_ffn_out_w"]).T),
        "w_down": feat(np.asarray(i["L0_ffn_ff_down_w"]).T),
        "w_up": f(np.asarray(i["L0_ffn_ff_up_w"]).T),
        "w_experts": feat(np.asarray(i["L0_ffn_expert_w"]).reshape(NE * D, D).T),
        "b_experts": f(np.asarray(i["L0_ffn_expert_b"]).reshape(-1)),
        "b_moe_out": f(np.asarray(i["L0_ffn_out_b"])),
        "b_up": f(np.asarray(i["L0_ffn_ff_up_b"])),
        "b_router": f(np.asarray(i["L0_ffn_router_b"])),
        "conv_w": f(np.asarray(i["L0_ffn_dw_kernel"]).reshape(NK, P, 3).transpose(1, 0, 2)),
        "conv_b": col(np.asarray(i["L0_ffn_dw_bias"])),
        "b_pw": col(np.asarray(i["L0_ffn_pw_b"])),
        "b_down": f(np.asarray(i["L0_ffn_ff_down_b"]).reshape(HID, 1)),
        "norm_w": f(np.asarray(i["L0_ffn_norm_w"])),
        "rope_q": rope_q,
        "rope_k": rope_k,
    }


def kernel(**inputs):
    import concourse.bacc as _bacc
    from concourse.bass_utils import run_bass_kernel_spmd as _run

    arrays = layouts(inputs)
    nc = _bacc.Bacc("TRN2", target_bir_lowering=False, num_devices=1)
    args = {k: nc.dram_tensor(f"in_{k}", v.shape, mybir.dt.from_np(v.dtype), kind="ExternalInput").ap()
            for k, v in arrays.items()}
    out = nc.dram_tensor("out_y", (B, P, NT, D), F32, kind="ExternalOutput").ap()
    build(nc, args, out)
    r = _run(nc, [{f"in_{k}": v for k, v in arrays.items()}], core_ids=[0])
    y = r.results[0]["out_y"]
    return np.ascontiguousarray(y.transpose(0, 2, 1, 3).reshape(B, T, D))
```

```python
import math

import numpy as np

import concourse.bass as bass
from concourse import mybir
from contextlib import ExitStack

F32 = mybir.dt.float32
F32R = mybir.dt.float32r
BF16 = mybir.dt.bfloat16
U32 = mybir.dt.uint32
U8 = mybir.dt.uint8
ALU = mybir.AluOpType
ACT = mybir.ActivationFunctionType
AX = mybir.AxisListType

B, T, D = 16, 256, 256
NH, NG, DH = 16, 4, 16
R = NH // NG
P = 128
NT, NK = T // P, D // P
NE, TOPK = 8, 2
HID = D // 4
HALF = DH // 2
LN_EPS, RMS_EPS = 1e-5, 1e-6

Q_TERMS = (0, 0, 1, 1, 0, 2)
K_TERMS = (0, 1, 0, 1, 2, 0)
MASK_ROW = len(Q_TERMS) * DH
MAX_ROW = MASK_ROW + 1
S_ROWS = MASK_ROW + 1
ST_ROWS = MAX_ROW + 3
MASKED = -float(2.0 ** 100)

W_SIZES = (("q", NK * D), ("out", NK * D), ("pw", NK * D), ("router", NK * NE), ("moe_out", NK * D),
           ("down", NK * P), ("up", D), ("experts", NK * NE * D))
W_AT, _at = {}, 0
for _name, _size in W_SIZES:
    W_AT[_name] = (_at, _at + _size)
    _at += _size
W_COLS = _at
EARLY = W_AT["q"][1]

B_EXPERTS, B_MOE_OUT, B_UP, B_ROUTER = 0, NE * D, NE * D + D, NE * D + 2 * D
B_COLS = B_ROUTER + NE

WORK_COLS = 2 * NG * 2 * T + 2 * 2 * T + 9 * NT * D + 8 * D + T
CHUNKS = 8
Q_DMAS, K_DMAS = 2 * len(Q_TERMS) + 1, len(K_TERMS) + 1


def rope_tables():
    theta = np.float32(10000.0) ** (-np.arange(0, DH, 2, dtype=np.float32) / np.float32(DH))
    angle = (np.arange(T, dtype=np.float32)[:, None] * theta[None, :].astype(np.float32)).astype(np.float32)
    cos, sin = np.cos(angle).astype(np.float32).T, np.sin(angle).astype(np.float32).T
    scale = np.float32(1.0 / math.sqrt(DH))
    cq, sq = np.repeat(cos, NH, axis=0) * scale, np.repeat(sin, NH, axis=0) * scale
    ck, sk = np.repeat(cos, NG, axis=0), np.repeat(sin, NG, axis=0)
    q = np.stack([cq, cq, sq, -sq], axis=1)
    k = np.stack([np.concatenate([ck, ck]), np.concatenate([sk, -sk])], axis=1)
    return np.ascontiguousarray(q.astype(np.float32)), np.ascontiguousarray(k.astype(np.float32))


def build(nc, a, out):
    ctx = ExitStack()

    def sb(name, shape, dt=F32):
        return ctx.enter_context(nc.sbuf_tensor(name, shape, dt))[:]

    def ps(name, shape, dt=F32):
        return ctx.enter_context(nc.psum_tensor(name, shape, dt))[:]

    def sem(name):
        return ctx.enter_context(nc.semaphore(name))

    with ctx:
        work = sb("work", [P, WORK_COLS])
        carved = [0]

        def carve(*dims):
            n = math.prod(dims)
            view = work[:, carved[0]:carved[0] + n]
            carved[0] += n
            if len(dims) == 1:
                return view
            names = "a b c".split()[:len(dims)]
            return view.rearrange(f"p ({' '.join(names)}) -> p {' '.join(names)}",
                                  **dict(zip(names[1:], dims[1:])))

        w_late = work[:, 0:W_COLS - EARLY]
        bias_f = work[0:3, W_COLS - EARLY:W_COLS - EARLY + B_COLS]
        bias_t = work[0:3, W_COLS - EARLY + B_COLS:W_COLS - EARLY + B_COLS + B_COLS // 2].bitcast(BF16)
        masks_at = W_COLS - EARLY + B_COLS + B_COLS // 2
        key_m, qry_m, key_pen = (work[0:B, masks_at + n * T:masks_at + (n + 1) * T] for n in range(3))
        w_q = sb("w_q", [P, NK * D])
        w_hi = sb("w_hi", [P, W_COLS], F32R)
        w_lo = sb("w_lo", [P, W_COLS], F32R)
        wk = sb("wk", [P, NK, P])
        wv = sb("wv", [P, NK, NG * DH])
        ident = sb("ident", [P, P])
        ident_r = sb("ident_r", [P, P], F32R)
        ident_b = sb("ident_b", [P, P], BF16)
        ones_b = sb("ones_b", [P, P], BF16)
        ones_f = sb("ones_f", [P, P])
        bias_rows = sb("bias_rows", [P, B_COLS], BF16)
        conv_w = sb("conv_w", [P, NK, 3])
        conv_b = sb("conv_b", [P, NK])
        pw_b = sb("pw_b", [P, NK])
        down_b = sb("down_b", [P, 1])
        norm_w = sb("norm_w", [P, D])
        rope_q = sb("rope_q", [P, 4, T])
        rope_k = sb("rope_k", [2 * NG * HALF, 2, T])
        iota8 = sb("iota8", [P, NE])
        minus_half = sb("minus_half", [P, NT])
        key_m8 = sb("key_m8", [B, T], U8)
        qry_m8 = sb("qry_m8", [B, T], U8)
        tok_m8 = sb("tok_m8", [P, B * NT], U8)
        tok_m = sb("tok_m", [P, B, NT])
        any_key = sb("any_key", [B, 1])
        any_diag = sb("any_diag", [B, B])
        key_row = sb("key_row", [B, T], BF16)
        alive_row = sb("alive_row", [B, T], BF16)
        key_dram = nc.dram_tensor("key_rows", (B, T), BF16).ap()
        alive_dram = nc.dram_tensor("alive_rows", (B, T), BF16).ap()
        alive_tok = sb("alive_tok", [P, B, NT])
        xin = sb("xin", [P, 2, NT, D])
        ctxin = sb("ctxin", [P, 2, NK, T])
        st1 = sb("st1", [P, NT, 6])
        mv1 = sb("mv1", [P, NT, 2])
        ve1 = sb("ve1", [P, NT])
        pw1 = sb("pw1", [P, NT])
        rstd1 = sb("rstd1", [P, NT])
        xn = sb("xn", [P, NT, D])
        xT_hi = sb("xT_hi", [P, NK, T], F32R)
        xT_lo = sb("xT_lo", [P, NK, T], F32R)
        rq1 = sb("rq1", [P, 2, T])
        rq2 = sb("rq2", [P, 2, T])
        rk1 = sb("rk1", [64, T])
        rk2 = sb("rk2", [64, T])
        qk = sb("qk", [P, 3, T])
        qk_r = sb("qk_r", [P, 3, T])
        qk_t = [sb(f"qk_t{n}", [P, 3, T], BF16) for n in range(3)]
        q_stack = sb("q_stack", [P, 2, NH, T], BF16)
        k_stack = sb("k_stack", [P, 2, NG, T], BF16)
        v_aug = sb("v_aug", [P, 2, NT, NG, 32])
        mx = sb("mx", [P, NT, NH])
        mx_r = sb("mx_r", [P, NT, NH])
        mx_t = sb("mx_t", [P, NT, P], BF16)
        mT = sb("mT", [3 * NH, T], BF16)
        probs = carve(2, NG, 2 * T)
        o_sb = carve(2, 2 * T)
        rec = sb("rec", [P, NT, NH])
        on = carve(NT, D)
        onT_hi = sb("onT_hi", [P, NK, T], F32R)
        onT_lo = sb("onT_lo", [P, NK, T], F32R)
        xres = sb("xres", [P, NT, D])
        x1 = sb("x1", [P, 2, NT, D])
        st2 = sb("st2", [P, NT, 6])
        mv2 = sb("mv2", [P, NT, 2])
        ve2 = sb("ve2", [P, NT])
        rstd2 = sb("rstd2", [P, NT])
        xn2 = sb("xn2", [P, NT, D])
        z = sb("z", [P, NK, T + 2])
        cv = carve(NK, T)
        cv_hi = sb("cv_hi", [P, NK, T], F32R)
        cv_lo = sb("cv_lo", [P, NK, T], F32R)
        sp_ = carve(NK, T)
        u = carve(NK, T)
        u_hi = sb("u_hi", [P, 2, NK, T], F32R)
        u_lo = sb("u_lo", [P, 2, NK, T], F32R)
        top_v = sb("top_v", [P, NT, 8])
        top_i = sb("top_i", [P, NT, 8], U32)
        top_f = sb("top_f", [P, NT, TOPK])
        top_d = sb("top_d", [P, NT])
        top_th = sb("top_th", [P, NT])
        top_w = sb("top_w", [P, TOPK, NT])
        hot = sb("hot", [P, NT, 2, NE])
        rw = sb("rw", [P, 2, NT, NE])
        ys = carve(4, 2, D)
        acc = carve(NT, D)
        sq = carve(NT, D)
        ssum = sb("ssum", [P, NT])
        ms3 = sb("ms3", [P, NT])
        rstd3 = sb("rstd3", [P, NT])
        h = carve(NT, D)
        hx = carve(NT, D)
        hT_hi = sb("hT_hi", [P, NK, T], F32R)
        hT_lo = sb("hT_lo", [P, NK, T], F32R)
        cT_hi, cT_lo = hT_hi, hT_lo
        gl = carve(T)
        gl_hi = sb("gl_hi", [P, T], F32R)
        gl_lo = sb("gl_lo", [P, T], F32R)
        y = carve(NT, D)

        sc = [ps(f"sc{n}", [P, 1024]) for n in range(2)]
        e_bank = [ps(f"e{n}", [P, 512]) for n in range(2)]
        g_bank = [ps(f"g{n}", [P, 512]) for n in range(2)]

        names = """w_in wq_in wk_in small_in mask_in bias_in rope_in pool_const id_ready w_hi_ready w_lo_ready early_hi early_lo
            const_ready ident_cast bias_step mask_step mask_ready any_mm alive_ready mask_rows_out
            x_in0 x_in1 ctx_in0 ctx_in1 ln1_stats ln1_mv ln1_ve ln1_pow ln1_rstd xn_ready xT_mm xT_hi_ready xT_lo_ready kv_mm q_mm
            rope_q_step rope_k_step q_ready k_ready v_ready t0_ready r1_ready t1_ready t2_ready q_stack_in k_stack_in
            s_mm max_ready m_step m_ready mT_mm mT_ready m_rows_in st_mm exp_ready pv_mm o_ready oT_mm rec_ready on_ready
            onT_mm onT_hi_ready onT_lo_ready att_mm xres_in x1_ready
            ln2_stats ln2_mv ln2_ve ln2_rstd xn2_ready x2T_mm z_ready tap_ready conv_step cv_hi_ready cv_lo_ready pw_mm sp_ready
            u_ready u_hi_ready u_lo_ready rt_mm topv_ready topi_ready topd_ready th_ready rw_step rw_ready
            ex_mm ys_ready comb_step cT_mm cT_hi_ready cT_lo_ready ow_mm sq_ready ms_ready rstd3_ready h_ready hx_ready
            hT_mm hT_hi_ready hT_lo_ready dn_mm gl_ready gl_hi_ready gl_lo_ready up_mm y_ready out_done dve_settled pool_settled""".split()
        S = {n: sem(n) for n in names}

        def wait(eng, name, value):
            if isinstance(value, int) and value <= 0:
                return
            eng.wait_ge(S[name], value)

        def settled(eng, name):
            eng.sem_inc(S[name], 1)

        def live(b):
            return not isinstance(b, int) or 0 <= b < B

        def pipeline(eng, body):
            for b in (-1, 0, 1, 2, 3):
                body(b, b % 2)
            with eng.Fori(4, B - 3, 2) as b:
                body(b, 0)
                body(b + 1, 1)
            for b in (B - 2, B - 1, B, B + 1, B + 2):
                body(b, b % 2)

        def w(part, which):
            lo, hi = W_AT[which]
            return part[:, lo:hi]

        def w_late_k(which):
            lo, hi = W_AT[which]
            return w_late[:, lo - EARLY:hi - EARLY].rearrange("p (k n) -> p k n", k=NK)

        def w_k(part, which):
            return w(part, which).rearrange("p (k n) -> p k n", k=NK)

        up_late = w_late[:, W_AT["up"][0] - EARLY:W_AT["up"][1] - EARLY]
        block = ctx.enter_context(nc.Block())

        @block.sync
        def _(sp):
            def load(b, p):
                wait(sp, "xn_ready", 2 * (b - 1))
                sp.dma_start(xin[:, p], a["x_tok"][b]).then_inc(S[f"x_in{p}"], 16)
                wait(sp, "kv_mm", b - 1)
                sp.dma_start(ctxin[:, p], a["ctx_T"][b]).then_inc(S[f"ctx_in{p}"], 16)

            sp.dma_start(xin[:, 0], a["x_tok"][0]).then_inc(S["x_in0"], 16)
            sp.dma_start(tok_m8, a["qmask_tok"]).then_inc(S["mask_in"], 16)
            sp.dma_start(key_m8, a["key_mask"]).then_inc(S["mask_in"], 16)
            sp.dma_start(qry_m8, a["qry_mask"]).then_inc(S["mask_in"], 16)
            sp.dma_start(w_q.rearrange("p (k n) -> p k n", k=NK), a["w_q"]).then_inc(S["wq_in"], 16)
            sp.dma_start(ctxin[:, 0], a["ctx_T"][0]).then_inc(S["ctx_in0"], 16)
            sp.wait_ge(S["const_ready"], 1)
            sp.dma_start(wk[:, :, 0:NG * DH], a["w_k"]).then_inc(S["wk_in"], 16)
            sp.dma_start(wv, a["w_v"]).then_inc(S["wk_in"], 16)
            sp.dma_start(rope_q, a["rope_q"]).then_inc(S["rope_in"], 16)
            sp.dma_start(rope_k, a["rope_k"]).then_inc(S["rope_in"], 16)
            sp.dma_start(bias_f[:, B_EXPERTS:B_MOE_OUT], a["b_experts"].partition_broadcast(3)).then_inc(S["bias_in"], 16)
            sp.dma_start(bias_f[:, B_MOE_OUT:B_UP], a["b_moe_out"].partition_broadcast(3)).then_inc(S["bias_in"], 16)
            sp.dma_start(bias_f[:, B_UP:B_ROUTER], a["b_up"].partition_broadcast(3)).then_inc(S["bias_in"], 16)
            sp.dma_start(bias_f[:, B_ROUTER:B_COLS], a["b_router"].partition_broadcast(3)).then_inc(S["bias_in"], 16)
            sp.dma_start(w_late_k("out"), a["w_out"]).then_inc(S["w_in"], 16)
            sp.dma_start(w_late_k("pw"), a["w_pw"]).then_inc(S["w_in"], 16)
            sp.dma_start(w_late_k("router"), a["w_router"]).then_inc(S["w_in"], 16)
            sp.dma_start(w_late_k("moe_out"), a["w_moe_out"]).then_inc(S["w_in"], 16)
            sp.dma_start(w_late_k("down")[:, :, 0:HID], a["w_down"]).then_inc(S["w_in"], 16)
            sp.dma_start(up_late[0:HID], a["w_up"]).then_inc(S["w_in"], 16)
            sp.dma_start(w_late_k("experts"), a["w_experts"]).then_inc(S["w_in"], 16)
            sp.dma_start(conv_w, a["conv_w"]).then_inc(S["small_in"], 16)
            sp.dma_start(conv_b, a["conv_b"]).then_inc(S["small_in"], 16)
            sp.dma_start(pw_b, a["b_pw"]).then_inc(S["small_in"], 16)
            sp.dma_start(down_b[0:HID], a["b_down"]).then_inc(S["small_in"], 16)
            sp.dma_start(norm_w, a["norm_w"].partition_broadcast(P)).then_inc(S["small_in"], 16)
            sp.wait_ge(S["mask_ready"], 2)
            sp.dma_start(key_dram, key_row).then_inc(S["mask_rows_out"], 16)
            sp.dma_start(alive_dram, alive_row).then_inc(S["mask_rows_out"], 16)
            sp.wait_ge(S["mask_rows_out"], 32)
            sp.wait_ge(S["const_ready"], 10)

            def body(b, p):
                o = 1 - p
                if live(b + 2):
                    load(b + 2, p)
                if live(b - 3):
                    wait(sp, "y_ready", b - 2)
                    sp.dma_start(out[b - 3], y).then_inc(S["out_done"], 16)
                if live(b):
                    wait(sp, "x1_ready", b)
                    sp.dma_start(xres, a["x_tok"][b]).then_inc(S["xres_in"], 16)
                    wait(sp, "mT_ready", b + 1)
                    sp.dma_start(q_stack[MAX_ROW:MAX_ROW + 3, p], mT).then_inc(S["m_rows_in"], 16)
                if live(b + 1):
                    n = b + 1
                    wait(sp, "st_mm", CHUNKS * b)
                    mask_q = alive_dram[bass.ds(n, 1)].unsqueeze(1).to_broadcast([1, NH, T])
                    mask_k = key_dram[bass.ds(n, 1)].unsqueeze(1).to_broadcast([1, NG, T])
                    sp.dma_start(q_stack[MASK_ROW:MASK_ROW + 1, o], mask_q).then_inc(S["q_stack_in"], 16)
                    sp.dma_start(k_stack[MASK_ROW:MASK_ROW + 1, o], mask_k).then_inc(S["k_stack_in"], 16)
                    for term, ready in ((0, "t0_ready"), (1, "t1_ready"), (2, "t2_ready")):
                        wait(sp, ready, n + 1)
                        for at, t in enumerate(K_TERMS):
                            if t == term:
                                sp.dma_start(k_stack[at * DH:(at + 1) * DH, o], qk_t[t][0:64, 2]).then_inc(S["k_stack_in"], 16)
                        for at, t in enumerate(Q_TERMS):
                            for half in range(2):
                                if t == term:
                                    row = at * DH + half * HALF
                                    sp.dma_start(q_stack[row:row + HALF, o], qk_t[t][:, half]).then_inc(S["q_stack_in"], 16)

            pipeline(sp, body)
            sp.wait_ge(S["out_done"], 16 * B)

        @block.gpsimd
        def _(pool):
            g = nc.gpsimd
            g.memset(ident, 0.0).then_inc(S["pool_const"], 1)
            pool.wait_ge(S["pool_const"], 1)
            g.affine_select(out=ident, in_=ident, compare_op=ALU.not_equal, fill=1.0, base=0,
                            pattern=[[-1, P]], channel_multiplier=1).then_inc(S["id_ready"], 1)
            g.memset(minus_half, -0.5).then_inc(S["id_ready"], 1)
            g.iota(iota8, pattern=[[1, NE]], base=0, channel_multiplier=0,
                   allow_small_or_imprecise_dtypes=True).then_inc(S["id_ready"], 1)
            pool.wait_ge(S["id_ready"], 3)

            def ln1_scale(n):
                wait(pool, "ln1_mv", 2 * n + 2)
                wait(pool, "xn_ready", 2 * n)
                settled(pool, "pool_settled")
                g.tensor_scalar(ve1, mv1[:, :, 1], LN_EPS, 1.0, ALU.add, ALU.mult).then_inc(S["ln1_ve"], 1)
                wait(pool, "ln1_ve", n + 1)
                g.tensor_tensor(pw1, ve1, minus_half, ALU.pow).then_inc(S["ln1_pow"], 1)
                if isinstance(n, int) and n == 0:
                    pool.wait_ge(S["alive_ready"], 1)
                wait(pool, "ln1_pow", n + 1)
                g.tensor_tensor(rstd1, pw1, alive_tok[:, bass.ds(n, 1)].rearrange("p o q -> p (o q)"),
                                ALU.mult).then_inc(S["ln1_rstd"], 1)

            def body(b, p):
                o = 1 - p
                Fr, M1, M2 = live(b + 1), live(b - 1), live(b - 2)
                m1, m2, n = b - 1, b - 2, b + 1
                if isinstance(b, int) and b == -1:
                    ln1_scale(0)
                if M1:
                    wait(pool, "ln2_ve", m1 + 1)
                    wait(pool, "xn2_ready", 2 * m1)
                    g.tensor_tensor(rstd2, ve2, minus_half, ALU.pow).then_inc(S["ln2_rstd"], 1)
                    wait(pool, "cv_hi_ready", m1 + 1)
                    wait(pool, "pw_mm", m1)
                    g.tensor_tensor(cv_lo, cv, cv_hi.bitcast(F32), ALU.subtract).then_inc(S["cv_lo_ready"], 1)
                if M1:
                    wait(pool, "sp_ready", 2 * m1 + 2)
                    wait(pool, "u_hi_ready", m1)
                    wait(pool, "u_lo_ready", m1)
                    g.tensor_tensor(u, z[:, :, 2:T + 2], sp_, ALU.add).then_inc(S["u_ready"], 1)
                if Fr:
                    wait(pool, "t0_ready", n + 1)
                    wait(pool, "t1_ready", n)
                    g.tensor_tensor(qk_r, qk, qk_t[0], ALU.subtract).then_inc(S["r1_ready"], 1)
                if M2:
                    wait(pool, "sq_ready", 2 * m2 + 2)
                    settled(pool, "pool_settled")
                    g.tensor_scalar(ms3, ssum, 1.0 / D, RMS_EPS, ALU.mult, ALU.add).then_inc(S["ms_ready"], 1)
                    wait(pool, "ms_ready", m2 + 1)
                    wait(pool, "h_ready", 2 * m2)
                    g.tensor_tensor(rstd3, ms3, minus_half, ALU.pow).then_inc(S["rstd3_ready"], 1)
                if live(b + 2):
                    ln1_scale(b + 2)
                if M1:
                    wait(pool, "topv_ready", 2 * m1 + 2)
                    g.tensor_tensor(top_d, top_v[:, :, 1], top_v[:, :, 0], ALU.subtract).then_inc(S["topd_ready"], 1)
                    wait(pool, "topi_ready", 2 * m1 + 2)
                    wait(pool, "rw_step", 7 * m1)
                    settled(pool, "pool_settled")
                    g.tensor_copy(top_f, top_i[:, :, 0:TOPK]).then_inc(S["rw_step"], 1)
                if Fr:
                    wait(pool, "t1_ready", n + 1)
                    wait(pool, "q_stack_in", 16 * Q_DMAS * n)
                    wait(pool, "k_stack_in", 16 * K_DMAS * n)
                    g.tensor_tensor(qk_t[2], qk_r, qk_t[1], ALU.subtract).then_inc(S["t2_ready"], 1)
                if M1:
                    wait(pool, "th_ready", m1 + 1)
                    settled(pool, "pool_settled")
                    g.tensor_scalar(top_w[:, 0], top_th, -0.5, 0.5, ALU.mult, ALU.add).then_inc(S["rw_step"], 1)
                    g.tensor_scalar(top_w[:, 1], top_th, 0.5, 0.5, ALU.mult, ALU.add).then_inc(S["rw_step"], 1)
                    wait(pool, "rw_step", 7 * m1 + 3)
                    wait(pool, "rw_ready", 2 * m1)
                    settled(pool, "pool_settled")
                    for q in range(NT):
                        for k in range(TOPK):
                            g.tensor_scalar(hot[:, q, k], iota8, top_f[:, q, k:k + 1], top_w[:, k, q:q + 1],
                                            ALU.is_equal, ALU.mult).then_inc(S["rw_step"], 1)
                    wait(pool, "rw_step", 7 * m1 + 7)
                    wait(pool, "comb_step", 16 * (m1 - 1))
                    for q in range(NT):
                        g.tensor_tensor(rw[:, o, q], hot[:, q, 0], hot[:, q, 1], ALU.add).then_inc(S["rw_ready"], 1)
                if M2:
                    wait(pool, "h_ready", 2 * m2 + 2)
                    wait(pool, "y_ready", m2)
                    g.tensor_tensor(hx, h, x1[:, p], ALU.add).then_inc(S["hx_ready"], 1)
                    wait(pool, "gl_hi_ready", m2 + 1)
                    wait(pool, "up_mm", m2)
                    g.tensor_tensor(gl_lo, gl, gl_hi.bitcast(F32), ALU.subtract).then_inc(S["gl_lo_ready"], 1)

            pipeline(pool, body)

        @block.scalar
        def _(act):
            s = nc.scalar
            act.wait_ge(S["id_ready"], 1)
            s.activation(ident_r, ident, ACT.Copy).then_inc(S["ident_cast"], 1)
            s.activation(ident_b, ident, ACT.Copy).then_inc(S["ident_cast"], 1)
            act.wait_ge(S["wq_in"], 16)
            s.activation(w(w_hi, "q"), w_q, ACT.Copy).then_inc(S["early_hi"], 1)

            def ys_chunk(b, e):
                m = b - 2
                wait(act, "ex_mm", CHUNKS * m + e + 1)
                wait(act, "comb_step", 16 * m + max(0, 4 * ((e - 4) // 2) + 4))
                s.activation(ys[:, e % 4].rearrange("p a d -> p (a d)"), e_bank[e % 2],
                             ACT.Silu).then_inc(S["ys_ready"], 1)

            def exp_chunk(b, c):
                r = c // 2
                wait(act, "st_mm", CHUNKS * b + c + 1)
                wait(act, "pv_mm", 4 * b + r - 1)
                s.activation(probs[:, r % 2, 2 * (c % 2):2 * (c % 2) + 2].rearrange("p g n -> p (g n)"), sc[c % 2],
                             ACT.Exp).then_inc(S["exp_ready"], 1)

            def copy(dst, src, done):
                s.activation(dst, src, ACT.Copy).then_inc(S[done], 1)

            def flat(x):
                return x.rearrange("p k n -> p (k n)")

            def body(b, p):
                o = 1 - p
                A, Fr, M1, M2 = live(b), live(b + 1), live(b - 1), live(b - 2)
                m1, m2, n = b - 1, b - 2, b + 1
                if Fr:
                    wait(act, "xT_mm", n + 1)
                    wait(act, "q_mm", n)
                    wait(act, "xT_lo_ready", n)
                    copy(flat(xT_hi), g_bank[0], "xT_hi_ready")
                if M2:
                    act.preload_act_table(ACT.Silu)
                    ys_chunk(b, 0)
                if M1:
                    wait(act, "onT_mm", m1 + 1)
                    wait(act, "att_mm", m1)
                    wait(act, "onT_lo_ready", m1)
                    copy(flat(onT_hi), g_bank[0], "onT_hi_ready")
                if M2:
                    for e in range(1, 4):
                        ys_chunk(b, e)
                    ys_chunk(b, 4)
                    ys_chunk(b, 5)
                if M1:
                    wait(act, "x2T_mm", m1 + 1)
                    wait(act, "u_ready", m1)
                    wait(act, "conv_step", 4 * m1)
                    s.activation(z[:, :, 2:T + 2], g_bank[0].rearrange("p (k n) -> p k n", k=NK),
                                 ACT.Copy).then_inc(S["z_ready"], 1)
                    if isinstance(b, int) and b == 1:
                        act.wait_ge(S["small_in"], 80)
                    wait(act, "cv_hi_ready", m1)
                    wait(act, "cv_lo_ready", m1)
                    for k in range(NK):
                        s.activation(cv[:, k], g_bank[0][:, k * T:(k + 1) * T], ACT.Identity, scale=conv_w[:, k, 2:3],
                                     bias=conv_b[:, k:k + 1]).then_inc(S["tap_ready"], 1)
                if M2:
                    ys_chunk(b, 6)
                if M1:
                    wait(act, "conv_step", 4 * m1 + 4)
                    wait(act, "pw_mm", m1)
                    wait(act, "cv_lo_ready", m1)
                    copy(flat(cv_hi), flat(cv), "cv_hi_ready")
                if M2:
                    ys_chunk(b, 7)
                if A:
                    wait(act, "mT_mm", b + 1)
                    wait(act, "m_rows_in", 16 * b)
                    copy(mT, g_bank[1].bitcast(BF16)[0:3 * NH, 0:T], "mT_ready")
                if M1:
                    if isinstance(b, int) and b == 1:
                        act.wait_ge(S["small_in"], 80)
                    wait(act, "pw_mm", m1 + 1)
                    for k in range(NK):
                        s.activation(sp_[:, k], g_bank[0][:, k * T:(k + 1) * T], ACT.Silu,
                                     bias=pw_b[:, k:k + 1]).then_inc(S["sp_ready"], 1)
                if A:
                    act.preload_act_table(ACT.Exp)
                    if isinstance(b, int) and b == 0:
                        act.wait_ge(S["bias_step"], 9)
                        act.wait_ge(S["w_lo_ready"], 1)
                    exp_chunk(b, 0)
                    exp_chunk(b, 1)
                if M2:
                    wait(act, "cT_mm", m2 + 1)
                    wait(act, "dn_mm", m2)
                    wait(act, "hT_lo_ready", m2)
                    copy(flat(cT_hi), e_bank[1], "cT_hi_ready")
                if Fr:
                    wait(act, "q_ready", n + 1)
                    wait(act, "k_ready", n + 1)
                    wait(act, "q_stack_in", 16 * Q_DMAS * n)
                    wait(act, "k_stack_in", 16 * K_DMAS * n)
                    copy(flat(qk_t[0]), flat(qk), "t0_ready")
                if isinstance(b, int) and b == -1:
                    act.wait_ge(S["w_in"], 16 * (len(W_SIZES) - 1))
                    act.wait_ge(S["const_ready"], 10)
                    copy(w_hi[:, EARLY:], w_late, "w_hi_ready")
                if M1:
                    wait(act, "u_ready", m1 + 1)
                    wait(act, "ow_mm", m1 - 1)
                    copy(flat(u_hi[:, o]), flat(u), "u_hi_ready")
                if A:
                    exp_chunk(b, 2)
                    exp_chunk(b, 3)
                if M2:
                    wait(act, "ow_mm", m2 + 1)
                    wait(act, "ms_ready", m2)
                    wait(act, "sq_ready", 2 * m2)
                    for q in range(NT):
                        s.activation(sq[:, q], e_bank[1][:, q * D:(q + 1) * D], ACT.Square,
                                     accum_out=ssum[:, q:q + 1]).then_inc(S["sq_ready"], 1)
                if Fr:
                    wait(act, "r1_ready", n + 1)
                    wait(act, "t2_ready", n)
                    copy(flat(qk_t[1]), flat(qk_r), "t1_ready")
                if A:
                    exp_chunk(b, 4)
                    exp_chunk(b, 5)
                if M1:
                    wait(act, "topd_ready", m1 + 1)
                    wait(act, "rw_step", 7 * m1)
                    s.activation(top_th, top_d, ACT.Tanh, scale=0.5).then_inc(S["th_ready"], 1)
                if A:
                    exp_chunk(b, 6)
                    exp_chunk(b, 7)
                if M2:
                    wait(act, "hT_mm", m2 + 1)
                    copy(flat(hT_hi), e_bank[1], "hT_hi_ready")
                    act.preload_act_table(ACT.Gelu)
                    wait(act, "dn_mm", m2 + 1)
                    wait(act, "gl_lo_ready", m2)
                    s.activation(gl, e_bank[1][:, 0:T], ACT.Gelu, bias=down_b[:, 0:1]).then_inc(S["gl_ready"], 1)
                    wait(act, "gl_ready", m2 + 1)
                    wait(act, "up_mm", m2)
                    copy(gl_hi, gl, "gl_hi_ready")

            pipeline(act, body)

        @block.vector
        def _(dve):
            v = nc.vector
            v.memset(wk, 0.0).then_inc(S["const_ready"], 1)

            def link(ins, name, value):
                ins.then_inc(S[name], 1)
                dve.wait_ge(S[name], value)

            dve.wait_ge(S["mask_in"], 48)
            v.tensor_copy(key_m, key_m8).then_inc(S["mask_step"], 1)
            v.tensor_copy(qry_m, qry_m8).then_inc(S["mask_step"], 1)
            link(v.tensor_copy(tok_m.rearrange("p b q -> p (b q)"), tok_m8), "mask_step", 3)
            link(v.tensor_reduce(any_key, key_m, axis=AX.X, op=ALU.max), "mask_step", 4)
            link(v.tensor_scalar(key_pen, key_m, -1.0, -MASKED, ALU.add, ALU.mult), "mask_step", 5)
            v.tensor_scalar(key_row, key_pen, any_key, None, ALU.mult).then_inc(S["mask_ready"], 1)
            v.tensor_scalar(alive_row, qry_m, any_key, None, ALU.mult).then_inc(S["mask_ready"], 1)
            v.memset(ones_f, 1.0).then_inc(S["mask_step"], 1)
            dve.wait_ge(S["id_ready"], 1)
            link(v.tensor_scalar(any_diag, ident[0:B, 0:B], any_key, None, ALU.mult), "mask_step", 7)
            dve.wait_ge(S["any_mm"], 1)
            v.tensor_tensor(alive_tok, tok_m, e_bank[0][:, 0:B].unsqueeze(2).to_broadcast([P, B, NT]),
                            ALU.mult).then_inc(S["alive_ready"], 1)
            v.memset(ones_b, 1.0).then_inc(S["const_ready"], 1)
            v.memset(bias_rows, 0.0).then_inc(S["bias_step"], 1)
            v.memset(down_b[HID:P], 0.0).then_inc(S["const_ready"], 1)
            v.memset(w_late_k("down")[:, :, HID:P], 0.0).then_inc(S["const_ready"], 1)
            v.memset(up_late[HID:P], 0.0).then_inc(S["const_ready"], 1)
            v.memset(qk, 0.0).then_inc(S["const_ready"], 1)
            v.memset(mx_t, 0.0).then_inc(S["const_ready"], 1)
            v.memset(z, 0.0).then_inc(S["const_ready"], 1)
            v.memset(k_stack[MASK_ROW:ST_ROWS], 1.0).then_inc(S["const_ready"], 1)
            v.memset(v_aug, 0.0).then_inc(S["const_ready"], 1)
            dve.wait_ge(S["const_ready"], 10)
            v.memset(v_aug[:, :, :, :, DH:DH + 1], 1.0).then_inc(S["const_ready"], 1)
            dve.wait_ge(S["const_ready"], 11)
            dve.wait_ge(S["early_hi"], 1)
            v.tensor_tensor(w(w_lo, "q"), w_q, w(w_hi, "q").bitcast(F32), ALU.subtract).then_inc(S["early_lo"], 1)

            def late_weights():
                dve.wait_ge(S["small_in"], 80)
                dve.wait_ge(S["w_in"], 16 * (len(W_SIZES) - 1))
                dve.wait_ge(S["w_hi_ready"], 1)
                v.tensor_tensor(w_lo[:, EARLY:], w_late, w_hi[:, EARLY:].bitcast(F32),
                                ALU.subtract).then_inc(S["w_lo_ready"], 1)

            def late_biases():
                dve.wait_ge(S["bias_in"], 64)
                for n in range(3):
                    link(v.tensor_copy(bias_t, bias_f), "bias_step", 3 * n + 2)
                    if n < 2:
                        link(v.tensor_tensor(bias_f, bias_f, bias_t, ALU.subtract), "bias_step", 3 * n + 3)
                    link(v.scalar_tensor_tensor(bias_rows[0:3], bias_t, ident[0:3, n:n + 1], bias_rows[0:3],
                                                ALU.mult, ALU.add), "bias_step", 3 * n + 4 if n < 2 else 9)

            def flat(x):
                return x.rearrange("p k n -> p (k n)")

            def lo_part(dst, src, hi, hi_ready, n, done):
                dve.wait_ge(S[hi_ready], n + 1)
                v.tensor_tensor(flat(dst), src, flat(hi).bitcast(F32), ALU.subtract).then_inc(S[done], 1)

            def maxima(b, c):
                q, g = c // NG, c % NG
                wait(dve, "s_mm", CHUNKS * b + c + 1)
                if c == 0:
                    wait(dve, "m_step", 3 * b)
                    wait(dve, "m_ready", b)
                v.tensor_reduce(mx[:, q, R * g:R * g + R], sc[(c + 1) % 2].rearrange("p (r n) -> p r n", r=R),
                                axis=AX.X, op=ALU.max).then_inc(S["max_ready"], 1)

            def combine(b, p, pair):
                m = b - 2
                wait(dve, "ys_ready", CHUNKS * m + 2 * pair + 2)
                if pair == 0:
                    wait(dve, "rw_ready", 2 * m + 2)
                    wait(dve, "cT_mm", m)
                for k in range(2):
                    for q in range(NT):
                        done = 16 * m + 4 * pair + 2 * k + q
                        src = ys[:, (2 * pair + q) % 4, k]
                        weight = rw[:, p, q, 2 * pair + k:2 * pair + k + 1]
                        if pair == 0 and k == 0:
                            v.tensor_scalar(acc[:, q], src, weight, None, ALU.mult).then_inc(S["comb_step"], 1)
                        else:
                            wait(dve, "comb_step", done - 1)
                            v.scalar_tensor_tensor(acc[:, q], src, weight, acc[:, q], ALU.mult,
                                                   ALU.add).then_inc(S["comb_step"], 1)

            def ln1_stats(n, h):
                wait(dve, f"x_in{h}", 8 * (n - h) + 16)
                wait(dve, "ln1_mv", 2 * n)
                for q in range(NT):
                    v.bn_stats(st1[:, q], xin[:, h, q]).then_inc(S["ln1_stats"], 1)
                wait(dve, "ln1_stats", 2 * n + 2)
                wait(dve, "ln1_ve", n)
                wait(dve, "xn_ready", 2 * n)
                settled(dve, "dve_settled")
                for q in range(NT):
                    v.bn_aggr(mv1[:, q], st1[:, q]).then_inc(S["ln1_mv"], 1)

            def ln1_apply(n, h):
                wait(dve, "ln1_mv", 2 * n + 2)
                wait(dve, "ln1_rstd", n + 1)
                wait(dve, "xT_mm", n)
                for q in range(NT):
                    v.tensor_scalar(xn[:, q], xin[:, h, q], mv1[:, q, 0:1], rstd1[:, q:q + 1], ALU.subtract,
                                    ALU.mult).then_inc(S["xn_ready"], 1)

            def body(b, p):
                o = 1 - p
                A, Fr, L1 = live(b), live(b + 1), live(b + 2)
                M1, M2, M3 = live(b - 1), live(b - 2), live(b - 3)
                m1, m2, m3, n = b - 1, b - 2, b - 3, b + 1
                if isinstance(b, int) and b == -1:
                    ln1_stats(0, 0)
                    ln1_apply(0, 0)
                if M1:
                    wait(dve, "pv_mm", 4 * m1 + 4)
                    wait(dve, "oT_mm", 2 * m1)
                    v.tensor_copy(o_sb[:, 1], g_bank[1]).then_inc(S["o_ready"], 1)
                    wait(dve, "on_ready", 2 * m1)
                    oq = [sc[0][:, q * 512:(q + 1) * 512].rearrange("p (r g d) -> p r g d", r=R, g=NG) for q in range(NT)]
                    for q in range(NT):
                        wait(dve, "oT_mm", 2 * m1 + q + 1)
                        v.reciprocal(rec[:, q].rearrange("p (r g) -> p r g", r=R), oq[q][:, :, :, DH]).then_inc(S["rec_ready"], 1)
                    wait(dve, "onT_mm", m1)
                    for q in range(NT):
                        wait(dve, "rec_ready", 2 * m1 + q + 1)
                        v.tensor_tensor(on[:, q].rearrange("p (g r d) -> p r g d", g=NG, r=R), oq[q][:, :, :, 0:DH],
                                        rec[:, q].rearrange("p (r g) -> p r g", r=R).unsqueeze(3).to_broadcast([P, R, NG, DH]),
                                        ALU.mult).then_inc(S["on_ready"], 1)
                if Fr:
                    wait(dve, "q_mm", n)
                    lo_part(xT_lo, g_bank[0], xT_hi, "xT_hi_ready", n, "xT_lo_ready")
                if isinstance(b, int) and b == -1:
                    late_biases()
                if M3:
                    wait(dve, "up_mm", m3 + 1)
                    wait(dve, "hx_ready", m3 + 1)
                    wait(dve, "out_done", 16 * m3)
                    v.tensor_tensor(flat(y), e_bank[1], flat(hx), ALU.add).then_inc(S["y_ready"], 1)
                if A:
                    maxima(b, 0)
                if M1:
                    wait(dve, "att_mm", m1)
                    lo_part(onT_lo, g_bank[0], onT_hi, "onT_hi_ready", m1, "onT_lo_ready")
                if A:
                    maxima(b, 1)
                if M1:
                    wait(dve, "att_mm", m1 + 1)
                    wait(dve, "xres_in", 16 * (m1 + 1))
                    wait(dve, "hx_ready", m1 - 1)
                    wait(dve, "xn2_ready", 2 * (m1 - 1))
                    v.tensor_tensor(flat(x1[:, o]), g_bank[1], flat(xres), ALU.add).then_inc(S["x1_ready"], 1)
                    wait(dve, "x1_ready", m1 + 1)
                    wait(dve, "ln2_mv", 2 * m1)
                    for q in range(NT):
                        v.bn_stats(st2[:, q], x1[:, o, q]).then_inc(S["ln2_stats"], 1)
                    wait(dve, "ln2_stats", 2 * m1 + 2)
                    wait(dve, "ln2_ve", m1)
                    wait(dve, "xn2_ready", 2 * m1)
                    settled(dve, "dve_settled")
                    for q in range(NT):
                        v.bn_aggr(mv2[:, q], st2[:, q]).then_inc(S["ln2_mv"], 1)
                    wait(dve, "ln2_mv", 2 * m1 + 2)
                    wait(dve, "ln2_rstd", m1)
                    v.tensor_scalar(ve2, mv2[:, :, 1], LN_EPS, None, ALU.add).then_inc(S["ln2_ve"], 1)
                if A:
                    maxima(b, 2)
                if M2:
                    combine(b, p, 0)
                if M1:
                    wait(dve, "ln2_rstd", m1 + 1)
                    wait(dve, "x2T_mm", m1)
                    for q in range(NT):
                        v.tensor_scalar(xn2[:, q], x1[:, o, q], mv2[:, q, 0:1], rstd2[:, q:q + 1], ALU.subtract,
                                        ALU.mult).then_inc(S["xn2_ready"], 1)
                if A:
                    maxima(b, 3)
                    maxima(b, 4)
                if M2:
                    combine(b, p, 1)
                if M1:
                    wait(dve, "z_ready", m1 + 1)
                    for tap in (1, 0):
                        for k in range(NK):
                            if tap == 1:
                                wait(dve, "tap_ready", 2 * m1 + k + 1)
                            else:
                                wait(dve, "conv_step", 4 * m1 + k + 1)
                            v.scalar_tensor_tensor(cv[:, k], z[:, k, tap:T + tap], conv_w[:, k, tap:tap + 1], cv[:, k],
                                                   ALU.mult, ALU.add).then_inc(S["conv_step"], 1)
                if A:
                    maxima(b, 5)
                    maxima(b, 6)
                    maxima(b, 7)
                    wait(dve, "max_ready", CHUNKS * (b + 1))
                    wait(dve, "mT_mm", b)
                    link(v.tensor_scalar(mx_t[:, :, 0:NH], mx, -1.0, None, ALU.mult), "m_step", 3 * b + 1)
                    link(v.scalar_tensor_tensor(mx_r, mx, -1.0, mx_t[:, :, 0:NH], ALU.mult, ALU.subtract),
                         "m_step", 3 * b + 2)
                    link(v.tensor_copy(mx_t[:, :, NH:2 * NH], mx_r), "m_step", 3 * b + 3)
                    v.tensor_tensor(mx_t[:, :, 2 * NH:3 * NH], mx_r, mx_t[:, :, NH:2 * NH],
                                    ALU.subtract).then_inc(S["m_ready"], 1)
                if M2:
                    combine(b, p, 2)
                    combine(b, p, 3)
                if Fr:
                    if isinstance(n, int) and n == 0:
                        dve.wait_ge(S["rope_in"], 32)
                    wait(dve, "q_mm", n + 1)
                    wait(dve, "q_ready", n)
                    qs = g_bank[1]
                    v.tensor_tensor(flat(rq1), qs, flat(rope_q[:, 0:2]), ALU.mult).then_inc(S["rope_q_step"], 1)
                    v.tensor_tensor(rq2[:, 1], qs[:, 0:T], rope_q[:, 2], ALU.mult).then_inc(S["rope_q_step"], 1)
                    v.tensor_tensor(rq2[:, 0], qs[:, T:2 * T], rope_q[:, 3], ALU.mult).then_inc(S["rope_q_step"], 1)
                if Fr:
                    if isinstance(n, int) and n == 0:
                        dve.wait_ge(S["rope_in"], 32)
                    wait(dve, "kv_mm", n + 1)
                    wait(dve, "k_ready", n)
                    ks = e_bank[0]
                    v.tensor_tensor(rk1, ks[0:64, 0:T], rope_k[:, 0], ALU.mult).then_inc(S["rope_k_step"], 1)
                    v.tensor_tensor(rk2[32:64], ks[0:32, 0:T], rope_k[0:32, 1], ALU.mult).then_inc(S["rope_k_step"], 1)
                    v.tensor_tensor(rk2[0:32], ks[32:64, 0:T], rope_k[32:64, 1], ALU.mult).then_inc(S["rope_k_step"], 1)
                    wait(dve, "pv_mm", 4 * (n - 1))
                    v.tensor_copy(v_aug[:, o, :, :, 0:DH],
                                  ks[:, T:T + NT * NG * DH].rearrange("p (t g d) -> p t g d", t=NT, g=NG)).then_inc(S["v_ready"], 1)
                    wait(dve, "rope_q_step", 3 * n + 3)
                    wait(dve, "t0_ready", n)
                    wait(dve, "r1_ready", n)
                    v.tensor_tensor(qk[:, 0:2], rq1, rq2, ALU.add).then_inc(S["q_ready"], 1)
                    wait(dve, "rope_k_step", 3 * n + 3)
                    wait(dve, "t0_ready", n)
                    wait(dve, "r1_ready", n)
                    v.tensor_tensor(qk[0:64, 2], rk1, rk2, ALU.add).then_inc(S["k_ready"], 1)
                if M2:
                    wait(dve, "dn_mm", m2)
                    lo_part(cT_lo, e_bank[1], cT_hi, "cT_hi_ready", m2, "cT_lo_ready")
                if M1:
                    wait(dve, "u_ready", m1 + 1)
                    lo_part(u_lo[:, o], flat(u), u_hi[:, o], "u_hi_ready", m1, "u_lo_ready")
                if L1:
                    ln1_stats(b + 2, p)
                if M2:
                    wait(dve, "rstd3_ready", m2 + 1)
                    wait(dve, "hT_mm", m2)
                    wait(dve, "hx_ready", m2)
                    for q in range(NT):
                        v.scalar_tensor_tensor(h[:, q], e_bank[1][:, q * D:(q + 1) * D], rstd3[:, q:q + 1], norm_w,
                                               ALU.mult, ALU.mult).then_inc(S["h_ready"], 1)
                if M1:
                    wait(dve, "rt_mm", m1 + 1)
                    wait(dve, "topd_ready", m1)
                    settled(dve, "dve_settled")
                    for q in range(NT):
                        v.max(top_v[:, q], g_bank[1][:, q * NE:(q + 1) * NE]).then_inc(S["topv_ready"], 1)
                    wait(dve, "topv_ready", 2 * m1 + 2)
                    wait(dve, "rw_step", 7 * m1)
                    settled(dve, "dve_settled")
                    for q in range(NT):
                        v.max_index(top_i[:, q], top_v[:, q], g_bank[1][:, q * NE:(q + 1) * NE]).then_inc(S["topi_ready"], 1)
                if A:
                    wait(dve, "pv_mm", 4 * b + 2)
                    wait(dve, "oT_mm", 2 * b)
                    v.tensor_copy(o_sb[:, 0], g_bank[0]).then_inc(S["o_ready"], 1)
                if L1:
                    ln1_apply(b + 2, p)
                if M2:
                    wait(dve, "ow_mm", m2 + 1)
                    lo_part(hT_lo, e_bank[1], hT_hi, "hT_hi_ready", m2, "hT_lo_ready")
                if isinstance(b, int) and b == -1:
                    late_weights()

            pipeline(dve, body)

        @block.tensor
        def _(pe):
            t = nc.tensor
            pe.wait_ge(S["mask_step"], 7)
            t.matmul(e_bank[0][:, 0:B], ones_f[0:B, :], any_diag, start=True, stop=True).then_inc(S["any_mm"], 1)
            pe.wait_ge(S["const_ready"], 11)
            pe.wait_ge(S["ident_cast"], 2)
            pe.wait_ge(S["id_ready"], 1)
            pe.wait_ge(S["alive_ready"], 1)

            def mm3(dst, l_hi, l_lo, r_hi, r_lo, start, stop):
                t.matmul(dst, l_hi, r_hi, start=start, stop=False)
                t.matmul(dst, l_hi, r_lo, start=False, stop=False)
                return t.matmul(dst, l_lo, r_hi, start=False, stop=stop)

            def bias(dst, at, n, stop=True):
                return t.matmul(dst, ones_b, bias_rows[:, at:at + n], start=False, stop=stop)

            def transposes(dst, src, done):
                for k in range(NK):
                    for q in range(NT):
                        last = t.transpose(dst[:, k * T + q * P:k * T + (q + 1) * P], src[:, q, k * P:(k + 1) * P], ident)
                last.then_inc(S[done], 1)

            def token_major(dst, l_hi, l_lo, which, q):
                for k in range(NK):
                    last = mm3(dst, l_hi[:, k, q * P:(q + 1) * P], l_lo[:, k, q * P:(q + 1) * P],
                               w_k(w_hi, which)[:, k], w_k(w_lo, which)[:, k], k == 0, k == NK - 1)
                return last

            def scores(b, p, c):
                q, g = c // NG, c % NG
                if c == 0:
                    wait(pe, "exp_ready", CHUNKS * b)
                    wait(pe, "q_stack_in", 16 * Q_DMAS * (b + 1))
                    wait(pe, "k_stack_in", 16 * K_DMAS * (b + 1))
                elif c == 1:
                    wait(pe, "on_ready", 2 * b)
                else:
                    wait(pe, "max_ready", CHUNKS * b + c - 1)
                for r in range(R):
                    last = t.matmul(sc[(c + 1) % 2][:, r * T:(r + 1) * T],
                                    q_stack[0:S_ROWS, p, R * g + r, q * P:(q + 1) * P],
                                    k_stack[0:S_ROWS, p, g], start=True, stop=True)
                last.then_inc(S["s_mm"], 1)

            def scores_T(b, p, r):
                half, kt = r // 2, r % 2
                for j in range(2):
                    c = 2 * r + j
                    if c == 0:
                        wait(pe, "m_rows_in", 16 * (b + 1))
                    elif c >= 2:
                        wait(pe, "exp_ready", CHUNKS * b + c - 1)
                    for i in range(2):
                        g = 2 * j + i
                        last = t.matmul(sc[c % 2][:, i * 512:(i + 1) * 512],
                                        k_stack[0:ST_ROWS, p, g, kt * P:(kt + 1) * P],
                                        q_stack[0:ST_ROWS, p, R * g + 2 * half:R * g + 2 * half + 2],
                                        start=True, stop=True)
                    last.then_inc(S["st_mm"], 1)

            def values(b, p, r):
                half, kt = r // 2, r % 2
                wait(pe, "exp_ready", CHUNKS * b + 2 * r + 2)
                if r == 0:
                    wait(pe, "sp_ready", 2 * b)
                elif r == 2:
                    wait(pe, "topi_ready", 2 * b)
                    if live(b + 1):
                        wait(pe, "rope_q_step", 3 * b + 6)
                for g in range(NG):
                    last = t.matmul(g_bank[half][32 * g:32 * g + 32], v_aug[:, p, kt, g], probs[:, r % 2, g],
                                    start=(kt == 0), stop=(kt == NT - 1))
                last.then_inc(S["pv_mm"], 1)

            def experts(b, p, e):
                m = b - 2
                q, ec = e % 2, e // 2
                if e == 0:
                    wait(pe, "ys_ready", CHUNKS * m)
                    if live(b):
                        wait(pe, "rope_k_step", 3 * b + 3)
                        wait(pe, "v_ready", b + 1)
                elif e == 1:
                    wait(pe, "y_ready", m)
                else:
                    wait(pe, "ys_ready", CHUNKS * m + e - 1)
                for k in range(NK):
                    at = slice(ec * 512, (ec + 1) * 512)
                    mm3(e_bank[e % 2], u_hi[:, p, k, q * P:(q + 1) * P], u_lo[:, p, k, q * P:(q + 1) * P],
                        w_k(w_hi, "experts")[:, k, at], w_k(w_lo, "experts")[:, k, at], k == 0, False)
                bias(e_bank[e % 2], B_EXPERTS + ec * 512, 512).then_inc(S["ex_mm"], 1)

            def body(b, p):
                o = 1 - p
                A, Fr = live(b), live(b + 1)
                M1, M2, M3 = live(b - 1), live(b - 2), live(b - 3)
                m1, m2, m3, n = b - 1, b - 2, b - 3, b + 1
                if M2:
                    experts(b, p, 0)
                if M1:
                    wait(pe, "o_ready", 2 * m1 + 2)
                    wait(pe, "exp_ready", CHUNKS * m1 + 8)
                    for q in range(NT):
                        for r in range(R):
                            last = t.transpose(sc[0][:, q * 512 + r * P:q * 512 + (r + 1) * P],
                                               o_sb[:, r // 2, (r % 2) * T + q * P:(r % 2) * T + (q + 1) * P], ident)
                        last.then_inc(S["oT_mm"], 1)
                if Fr:
                    wait(pe, "xn_ready", 2 * n + 2)
                    wait(pe, "o_ready", 2 * b - 1)
                    transposes(g_bank[0], xn, "xT_mm")
                if M3:
                    wait(pe, "gl_lo_ready", m3 + 1)
                    wait(pe, "gl_ready", m3 + 1)
                    for q in range(NT):
                        at = e_bank[1][:, q * D:(q + 1) * D]
                        mm3(at, gl_hi[:, q * P:(q + 1) * P], gl_lo[:, q * P:(q + 1) * P], w(w_hi, "up"), w(w_lo, "up"),
                            True, False)
                        last = bias(at, B_UP, D)
                    last.then_inc(S["up_mm"], 1)
                if A:
                    scores(b, p, 0)
                if M1:
                    wait(pe, "on_ready", 2 * m1 + 2)
                    if Fr:
                        wait(pe, "xT_lo_ready", n + 1)
                    transposes(g_bank[0], on, "onT_mm")
                if M2:
                    experts(b, p, 1)
                if A:
                    scores(b, p, 1)
                if M2:
                    experts(b, p, 2)
                if M1:
                    if isinstance(b, int) and b == 1:
                        pe.wait_ge(S["w_lo_ready"], 1)
                        pe.wait_ge(S["bias_step"], 9)
                    wait(pe, "onT_lo_ready", m1 + 1)
                    for q in range(NT):
                        last = token_major(g_bank[1][:, q * D:(q + 1) * D], onT_hi, onT_lo, "out", q)
                    last.then_inc(S["att_mm"], 1)
                if A:
                    scores(b, p, 2)
                if M2:
                    experts(b, p, 3)
                if A:
                    scores(b, p, 3)
                if M2:
                    experts(b, p, 4)
                if A:
                    scores(b, p, 4)
                if M2:
                    experts(b, p, 5)
                if M1:
                    wait(pe, "xn2_ready", 2 * m1 + 2)
                    transposes(g_bank[0], xn2, "x2T_mm")
                if A:
                    scores(b, p, 5)
                    scores(b, p, 6)
                if M2:
                    experts(b, p, 6)
                if Fr:
                    wait(pe, f"ctx_in{o}", 8 * (n - o) + 16)
                    if isinstance(n, int) and n == 0:
                        pe.wait_ge(S["wk_in"], 32)
                    if M2:
                        wait(pe, "ys_ready", CHUNKS * m2 + 7)
                    else:
                        wait(pe, "v_ready", n)
                        wait(pe, "rope_k_step", 3 * n)
                    for k in range(NK):
                        t.matmul(e_bank[0][:, 0:T], wk[:, k], ctxin[:, o, k], start=(k == 0), stop=(k == NK - 1))
                    for kt in range(NT):
                        at = e_bank[0][:, T + kt * 64:T + (kt + 1) * 64]
                        for k in range(NK):
                            last = t.matmul(at, ctxin[:, o, k, kt * P:(kt + 1) * P], wv[:, k], start=(k == 0),
                                            stop=(k == NK - 1))
                    last.then_inc(S["kv_mm"], 1)
                if A:
                    scores(b, p, 7)
                if M2:
                    experts(b, p, 7)
                if A:
                    wait(pe, "m_ready", b + 1)
                    wait(pe, "x1_ready", b)
                    for q in range(NT):
                        last = t.transpose(g_bank[1].bitcast(BF16)[:, q * P:(q + 1) * P], mx_t[:, q], ident_b)
                    last.then_inc(S["mT_mm"], 1)
                if M1:
                    wait(pe, "cv_lo_ready", m1 + 1)
                    wait(pe, "tap_ready", 2 * m1 + 2)
                    for half in range(NK):
                        for k in range(NK):
                            at = slice(half * P, (half + 1) * P)
                            last = mm3(g_bank[0][:, half * T:(half + 1) * T], w_k(w_hi, "pw")[:, k, at],
                                       w_k(w_lo, "pw")[:, k, at], cv_hi[:, k], cv_lo[:, k], k == 0, k == NK - 1)
                    last.then_inc(S["pw_mm"], 1)
                if Fr:
                    wait(pe, "xT_lo_ready", n + 1)
                    wait(pe, "mT_ready", b + 1)
                    if isinstance(n, int) and n == 0:
                        pe.wait_ge(S["early_lo"], 1)
                    for half in range(2):
                        for k in range(NK):
                            at = slice(half * P, (half + 1) * P)
                            last = mm3(g_bank[1][:, half * T:(half + 1) * T], w_k(w_hi, "q")[:, k, at],
                                       w_k(w_lo, "q")[:, k, at], xT_hi[:, k], xT_lo[:, k], k == 0, k == NK - 1)
                    last.then_inc(S["q_mm"], 1)
                if A:
                    scores_T(b, p, 0)
                if M2:
                    wait(pe, "comb_step", 16 * m2 + 16)
                    wait(pe, "ys_ready", CHUNKS * m2 + 8)
                    transposes(e_bank[1], acc, "cT_mm")
                if A:
                    scores_T(b, p, 1)
                    values(b, p, 0)
                if M2:
                    wait(pe, "cT_lo_ready", m2 + 1)
                    for q in range(NT):
                        at = e_bank[1][:, q * D:(q + 1) * D]
                        for k in range(NK):
                            mm3(at, cT_hi[:, k, q * P:(q + 1) * P], cT_lo[:, k, q * P:(q + 1) * P],
                                w_k(w_hi, "moe_out")[:, k], w_k(w_lo, "moe_out")[:, k], k == 0, False)
                        for k in range(NK):
                            for part in (u_hi, u_lo):
                                t.matmul(at[:, k * P:(k + 1) * P], part[:, p, k, q * P:(q + 1) * P], ident_r,
                                         start=False, stop=False)
                        last = bias(at, B_MOE_OUT, D)
                    last.then_inc(S["ow_mm"], 1)
                if A:
                    scores_T(b, p, 2)
                if M1:
                    wait(pe, "u_lo_ready", m1 + 1)
                    wait(pe, "x1_ready", m1 + 1)
                    if Fr:
                        wait(pe, "rope_q_step", 3 * n + 3)
                    elif A:
                        wait(pe, "mT_ready", b + 1)
                    for q in range(NT):
                        at = g_bank[1][:, q * NE:(q + 1) * NE]
                        for k in range(NK):
                            mm3(at, u_hi[:, o, k, q * P:(q + 1) * P], u_lo[:, o, k, q * P:(q + 1) * P],
                                w_k(w_hi, "router")[:, k], w_k(w_lo, "router")[:, k], k == 0, False)
                        last = bias(at, B_ROUTER, NE)
                    last.then_inc(S["rt_mm"], 1)
                if A:
                    values(b, p, 1)
                    scores_T(b, p, 3)
                    values(b, p, 2)
                if M2:
                    wait(pe, "h_ready", 2 * m2 + 2)
                    transposes(e_bank[1], h, "hT_mm")
                if A:
                    values(b, p, 3)
                if M2:
                    wait(pe, "hT_lo_ready", m2 + 1)
                    for k in range(NK):
                        last = mm3(e_bank[1][:, 0:T], w_k(w_hi, "down")[:, k], w_k(w_lo, "down")[:, k], hT_hi[:, k],
                                   hT_lo[:, k], k == 0, k == NK - 1)
                    last.then_inc(S["dn_mm"], 1)

            pipeline(pe, body)


def layouts(i):
    f = lambda x: np.ascontiguousarray(x)
    x = np.asarray(i["x"])
    feat = lambda wt: f(wt.reshape(NK, P, -1).transpose(1, 0, 2))
    col = lambda v: f(v.reshape(NK, P).T)
    w_q = np.asarray(i["L0_xattn_w_q"]).reshape(D, NH, 2, HALF).transpose(0, 2, 3, 1).reshape(D, D)
    w_k = np.asarray(i["L0_xattn_w_k"]).reshape(D, NG, 2, HALF).transpose(0, 2, 3, 1).reshape(D, NG * DH)
    rope_q, rope_k = rope_tables()
    key_mask = np.asarray(i["mask_BxS2_bk0"])
    qry_mask = np.asarray(i["mask_BxS2_bf1"])
    return {
        "x_tok": f(x.reshape(B, NT, P, D).transpose(0, 2, 1, 3)),
        "ctx_T": f(np.asarray(i["ctx_1024"]).transpose(0, 2, 1).reshape(B, NK, P, T).transpose(0, 2, 1, 3)),
        "key_mask": f(key_mask),
        "qry_mask": f(qry_mask),
        "qmask_tok": f(qry_mask.reshape(B, NT, P).transpose(2, 0, 1).reshape(P, B * NT)),
        "w_q": feat(w_q),
        "w_k": feat(w_k),
        "w_v": feat(np.asarray(i["L0_xattn_w_v"])),
        "w_out": feat(np.asarray(i["L0_xattn_w_out"])),
        "w_pw": feat(np.asarray(i["L0_ffn_pw_w"]).T),
        "w_router": feat(np.asarray(i["L0_ffn_router_w"]).T),
        "w_moe_out": feat(np.asarray(i["L0_ffn_out_w"]).T),
        "w_down": feat(np.asarray(i["L0_ffn_ff_down_w"]).T),
        "w_up": f(np.asarray(i["L0_ffn_ff_up_w"]).T),
        "w_experts": feat(np.asarray(i["L0_ffn_expert_w"]).reshape(NE * D, D).T),
        "b_experts": f(np.asarray(i["L0_ffn_expert_b"]).reshape(-1)),
        "b_moe_out": f(np.asarray(i["L0_ffn_out_b"])),
        "b_up": f(np.asarray(i["L0_ffn_ff_up_b"])),
        "b_router": f(np.asarray(i["L0_ffn_router_b"])),
        "conv_w": f(np.asarray(i["L0_ffn_dw_kernel"]).reshape(NK, P, 3).transpose(1, 0, 2)),
        "conv_b": col(np.asarray(i["L0_ffn_dw_bias"])),
        "b_pw": col(np.asarray(i["L0_ffn_pw_b"])),
        "b_down": f(np.asarray(i["L0_ffn_ff_down_b"]).reshape(HID, 1)),
        "norm_w": f(np.asarray(i["L0_ffn_norm_w"])),
        "rope_q": rope_q,
        "rope_k": rope_k,
    }


def kernel(**inputs):
    import concourse.bacc as _bacc
    from concourse.bass_utils import run_bass_kernel_spmd as _run

    arrays = layouts(inputs)
    nc = _bacc.Bacc("TRN2", target_bir_lowering=False, num_devices=1)
    args = {k: nc.dram_tensor(f"in_{k}", v.shape, mybir.dt.from_np(v.dtype), kind="ExternalInput").ap()
            for k, v in arrays.items()}
    out = nc.dram_tensor("out_y", (B, P, NT, D), F32, kind="ExternalOutput").ap()
    build(nc, args, out)
    r = _run(nc, [{f"in_{k}": v for k, v in arrays.items()}], core_ids=[0])
    y = r.results[0]["out_y"]
    return np.ascontiguousarray(y.transpose(0, 2, 1, 3).reshape(B, T, D))
```
